# Optimizing a Trainium2 kernel written in Bass

```python
import numpy as np
import jax
import jax.numpy as jnp

def _softmax(x, axis=-1):
    return jax.nn.softmax(x, axis=axis)

def _gelu(x):
    return jax.nn.gelu(x, approximate=True)

def _silu(x):
    return jax.nn.silu(x)

def _sigmoid(x):
    return jax.nn.sigmoid(x)

def _layernorm(x, axis=-1, eps=1e-05):
    m = jnp.mean(x, axis=axis, keepdims=True)
    v = jnp.var(x, axis=axis, keepdims=True)
    return (x - m) / jnp.sqrt(v + eps)

def _scatter_add(tgt, idx, src, axis=0):
    return tgt.at[idx].add(src)

def _segment_sum(src, seg, n):
    return jax.ops.segment_sum(src, seg, n)
kernel_name = 'mk_prb_d1_jaxref_r8_33e034'

def setup_inputs(seed: int=0):
    np.random.seed(seed)
    _w = jnp.asarray

    def _L0_attn_setup():
        import jax, jax.numpy as jnp
        import numpy as np
        B, N, DIM = (2, 256, 128)
        HEADS, DHEAD = (16, 64)
        GNN_DEPTH = 2
        EPS = 1e-05

        def layer_norm(x, gamma):
            mu = jnp.mean(x, axis=-1, keepdims=True)
            var = jnp.var(x, axis=-1, keepdims=True)
            return (x - mu) / jnp.sqrt(var + EPS) * gamma
        key = jax.random.key(seed)
        ks = jax.random.split(key, 12)
        hd = HEADS * DHEAD
        s = lambda fan: 1.0 / np.sqrt(fan)
        return {'x': jax.random.normal(ks[0], (B, N, DIM), dtype=jnp.float32), 'gamma_in': jnp.ones((DIM,), dtype=jnp.float32), 'Wq': jax.random.normal(ks[1], (DIM, hd), dtype=jnp.float32) * s(DIM), 'Wk': jax.random.normal(ks[2], (DIM, hd), dtype=jnp.float32) * s(DIM), 'Wv': jax.random.normal(ks[3], (DIM, hd), dtype=jnp.float32) * s(DIM), 'gnn_w': jax.random.normal(ks[4], (GNN_DEPTH, DHEAD, DHEAD), dtype=jnp.float32) * s(DHEAD), 'gnn_b': jnp.zeros((GNN_DEPTH, DHEAD), dtype=jnp.float32), 'lin_w': jax.random.normal(ks[5], (DHEAD, DHEAD), dtype=jnp.float32) * s(DHEAD), 'lin_b': jnp.zeros((DHEAD,), dtype=jnp.float32), 'Wo': jax.random.normal(ks[6], (hd, DIM), dtype=jnp.float32) * s(hd), 'gamma_out': jnp.ones((DIM,), dtype=jnp.float32)}
    _L0_attn_in = _L0_attn_setup()

    def _L0_ffn_setup():
        import jax, jax.numpy as jnp
        import numpy as np
        D_MODEL, FF_DIM = (128, 256)
        N_SHARED, N_ROUTED, TOP_K = (1, 8, 2)
        BATCH, SEQ = (2, 256)
        key = jax.random.key(seed)
        ks = jax.random.split(key, 8)
        init = lambda k, shape: jax.random.normal(k, shape, jnp.float32) * 0.02
        x = jax.random.normal(ks[0], (BATCH, SEQ, D_MODEL), jnp.float32)
        Wg = init(ks[1], (D_MODEL, N_ROUTED))
        Ws1 = init(ks[2], (D_MODEL, FF_DIM))
        Ws3 = init(ks[3], (D_MODEL, FF_DIM))
        Ws2 = init(ks[4], (FF_DIM, D_MODEL))
        We1 = init(ks[5], (N_ROUTED, D_MODEL, FF_DIM))
        We3 = init(ks[6], (N_ROUTED, D_MODEL, FF_DIM))
        We2 = init(ks[7], (N_ROUTED, FF_DIM, D_MODEL))
        return {'x': x, 'Wg': Wg, 'Ws1': Ws1, 'Ws3': Ws3, 'Ws2': Ws2, 'We1': We1, 'We3': We3, 'We2': We2}
    _L0_ffn_in = _L0_ffn_setup()
    _d = {'L0_attn_x': _L0_attn_in['x'], 'L0_attn_gamma_in': _L0_attn_in['gamma_in'], 'L0_attn_Wq': _L0_attn_in['Wq'], 'L0_attn_Wk': _L0_attn_in['Wk'], 'L0_attn_Wv': _L0_attn_in['Wv'], 'L0_attn_gnn_w': _L0_attn_in['gnn_w'], 'L0_attn_gnn_b': _L0_attn_in['gnn_b'], 'L0_attn_lin_w': _L0_attn_in['lin_w'], 'L0_attn_lin_b': _L0_attn_in['lin_b'], 'L0_attn_Wo': _L0_attn_in['Wo'], 'L0_attn_gamma_out': _L0_attn_in['gamma_out'], 'L0_ffn_Wg': _L0_ffn_in['Wg'], 'L0_ffn_Ws1': _L0_ffn_in['Ws1'], 'L0_ffn_Ws3': _L0_ffn_in['Ws3'], 'L0_ffn_Ws2': _L0_ffn_in['Ws2'], 'L0_ffn_We1': _L0_ffn_in['We1'], 'L0_ffn_We3': _L0_ffn_in['We3'], 'L0_ffn_We2': _L0_ffn_in['We2']}
    _x0 = _d['L0_attn_x']
    _d['L0_attn_x'] = jax.random.normal(jax.random.fold_in(jax.random.key(seed), 1), (8, 256, 128), dtype=_x0.dtype)
    del _x0
    return _d

def reference(L0_attn_x, L0_attn_gamma_in, L0_attn_Wq, L0_attn_Wk, L0_attn_Wv, L0_attn_gnn_w, L0_attn_gnn_b, L0_attn_lin_w, L0_attn_lin_b, L0_attn_Wo, L0_attn_gamma_out, L0_ffn_Wg, L0_ffn_Ws1, L0_ffn_Ws3, L0_ffn_Ws2, L0_ffn_We1, L0_ffn_We3, L0_ffn_We2):

    def _L0_attn_ref(x, gamma_in, Wq, Wk, Wv, gnn_w, gnn_b, lin_w, lin_b, Wo, gamma_out):
        import jax, jax.numpy as jnp
        import numpy as np
        B, N, DIM = (2, 256, 128)
        HEADS, DHEAD = (16, 64)
        GNN_DEPTH = 2
        EPS = 1e-05

        def layer_norm(x, gamma):
            mu = jnp.mean(x, axis=-1, keepdims=True)
            var = jnp.var(x, axis=-1, keepdims=True)
            return (x - mu) / jnp.sqrt(var + EPS) * gamma
        b, n, _ = x.shape
        scale = DHEAD ** (-0.5)
        xn = layer_norm(x, gamma_in)
        q = (xn @ Wq).reshape(b, n, HEADS, DHEAD).transpose(0, 2, 1, 3) * scale
        k = (xn @ Wk).reshape(b, n, HEADS, DHEAD).transpose(0, 2, 1, 3)
        v = (xn @ Wv).reshape(b, n, HEADS, DHEAD).transpose(0, 2, 1, 3)
        sim = jnp.einsum('bhid,bhjd->bhij', q, k)
        mask_value = -jnp.finfo(sim.dtype).max
        causal_mask = jnp.triu(jnp.ones((n, n), dtype=bool), k=1)
        sim = jnp.where(causal_mask, mask_value, sim)
        attn = jax.nn.softmax(sim.astype(jnp.float32), axis=-1)
        out = jnp.einsum('bhij,bhjd->bhid', attn, v)
        adj = attn.reshape(b * HEADS, n, n)
        adj = jnp.clip(adj + jnp.eye(n, dtype=adj.dtype), 0.0, 1.0)
        deg = jnp.sum(adj, axis=-1, keepdims=True)
        feats = v.reshape(b * HEADS, n, DHEAD)
        for l in range(GNN_DEPTH):
            h = feats @ gnn_w[l] + gnn_b[l]
            h = jnp.einsum('bij,bjd->bid', adj, h) / deg
            feats = jax.nn.gelu(h + feats, approximate=False)
        gnn_out = feats @ lin_w + lin_b
        out = out + gnn_out.reshape(b, HEADS, n, DHEAD)
        out = out.transpose(0, 2, 1, 3).reshape(b, n, HEADS * DHEAD)
        return layer_norm(out @ Wo, gamma_out)

    def _L0_ffn_ref(x, Wg, Ws1, Ws3, Ws2, We1, We3, We2):
        import jax, jax.numpy as jnp
        import numpy as np
        D_MODEL, FF_DIM = (128, 256)
        N_SHARED, N_ROUTED, TOP_K = (1, 8, 2)
        BATCH, SEQ = (2, 256)
        B, S, d = x.shape
        E = Wg.shape[1]
        xf = x.reshape(-1, d)
        T = xf.shape[0]
        gates = jax.nn.sigmoid(xf @ Wg)
        vals, idx = jax.lax.top_k(gates, TOP_K)
        vals = vals / vals.sum(axis=-1, keepdims=True)
        w = jnp.zeros((T, E), x.dtype).at[jnp.arange(T)[:, None], idx].add(vals)
        shared = jax.nn.silu(xf @ Ws1) * (xf @ Ws3) @ Ws2
        h = jax.nn.silu(jnp.einsum('td,edf->tef', xf, We1)) * jnp.einsum('td,edf->tef', xf, We3)
        routed = jnp.einsum('tef,efd,te->td', h, We2, w)
        out = (shared + routed) / (N_SHARED + TOP_K)
        return out.reshape(B, S, d)
    x = L0_attn_x
    xn = _layernorm(x, axis=-1)
    x = x + _L0_attn_ref(xn, L0_attn_gamma_in, L0_attn_Wq, L0_attn_Wk, L0_attn_Wv, L0_attn_gnn_w, L0_attn_gnn_b, L0_attn_lin_w, L0_attn_lin_b, L0_attn_Wo, L0_attn_gamma_out) + _L0_ffn_ref(xn, L0_ffn_Wg, L0_ffn_Ws1, L0_ffn_Ws3, L0_ffn_Ws2, L0_ffn_We1, L0_ffn_We3, L0_ffn_We2)
    return x

_drawn_inputs = setup_inputs


def setup_inputs(seed=0):
    import zlib

    import numpy as np

    out = dict(_drawn_inputs(seed))
    spreads = {'L0_attn_gamma_in': (1.0, 0.2),
     'L0_attn_gnn_b': (0.0, 0.1),
     'L0_attn_lin_b': (0.0, 0.1),
     'L0_attn_gamma_out': (1.0, 0.2)}
    factors = {'L0_ffn_Wg': 8.0,
     'L0_ffn_Ws1': 8.0,
     'L0_ffn_Ws3': 8.0,
     'L0_ffn_Ws2': 8.0,
     'L0_ffn_We1': 8.0,
     'L0_ffn_We3': 8.0,
     'L0_ffn_We2': 8.0}
    for name, (base, spread) in spreads.items():
        noise = np.random.default_rng([zlib.crc32(name.encode()), seed]).standard_normal(out[name].shape)
        drawn = base * np.exp(spread * noise) if base else spread * noise
        out[name] = jnp.asarray(drawn.astype(out[name].dtype))
    for name, factor in factors.items():
        out[name] = (out[name] * factor).astype(out[name].dtype)
    return out
```

```python
from contextlib import ExitStack

import concourse.bass as bass
from concourse import mybir
from concourse.alu_op_type import AluOpType as ALU

F32 = mybir.dt.float32
U32 = mybir.dt.uint32
ACT = mybir.ActivationFunctionType
AX_X = mybir.AxisListType.X

P = 128
T = 2
H, DH = 16, 64
PAIRS = H // 2
E = 9
C = 2
VHW = 2 * DH + 2
BANKS = 8
EPS = 1e-5
MASKED = -3.0e38


def product_jobs():
    jobs = [("gates", 0), ("qm", 0)]
    for s in range(PAIRS):
        jobs += [("scores", 2 * s), ("scores", 2 * s + 1)]
        if s + 1 < PAIRS:
            jobs.append(("qm", s + 1))
        jobs.append(("vh", s))
        if s >= 1:
            jobs += [("turn", 2 * s - 2), ("turn", 2 * s - 1)]
        if s >= 2:
            jobs += [("layer1", 2 * s - 4), ("layer1", 2 * s - 3)]
    up = lambda e: [("gate_up", e), ("up", e)]
    jobs += up(0) + [("turn", H - 2), ("turn", H - 1), ("layer1", H - 4), ("layer1", H - 3)]
    jobs += up(1) + [("layer1", H - 2), ("layer1", H - 1)]
    jobs += up(2) + [("down", 0)] + up(3) + [("down", 1)] + up(4) + [("down", 2)] + up(5) + [("down", 3)]
    jobs += [("layer2", 0), ("layer2", 1)] + up(6) + [("weigh2", 0), ("weigh2", 1)]
    jobs += [("layer2", 2), ("layer2", 3), ("down", 4)] + up(7) + [("weigh2", 2), ("weigh2", 3), ("down", 5)]
    jobs += up(8) + [("stack", p) for p in range(4)] + [("down", 6), ("x_turn", 0)]
    jobs += [("stack", 4), ("down", 7)] + [("stack", p) for p in range(5, 8)]
    jobs += [("down", 8), ("out", 0), ("out_turn", 0)]
    return jobs


JOBS = product_jobs()
SLOTS = -(-len(JOBS) // BANKS) * BANKS

READ_BY = {
    "gates": "gates_taken", "qm": "qm_copied", "vh": "vh_copied", "scores": "scores_masked",
    "turn": "et_copied", "layer1": "layer1_copied", "gate_up": "silu_made", "up": "hidden_made",
    "down": "down_added", "layer2": "z_copied", "weigh2": "weigh2_scaled", "stack": "stack_copied",
    "x_turn": "xt_copied", "out": "y_copied", "out_turn": "y_normed",
}

VECTOR_LINKS = 30

PER_SEQ = {
    "gates": 1, "qm": PAIRS, "vh": PAIRS, "scores": H, "turn": H, "layer1": H, "gate_up": E, "up": E,
    "down": E, "layer2": 4, "weigh2": 4, "stack": PAIRS, "x_turn": 1, "out": 1, "out_turn": 1,
    "gates_taken": 1, "qm_copied": PAIRS, "exp_done": 2 * H, "et_copied": H, "layer1_copied": H,
    "tanh_done": E, "gelu1_done": 2, "z_copied": 4, "gelu2_done": 2, "stack_copied": PAIRS,
    "xt_copied": 2, "y_copied": 1,
    "vh_copied": PAIRS, "scores_masked": H, "negmax_done": PAIRS, "diag_set": PAIRS, "silu_made": E,
    "hidden_made": E, "down_added": E, "norms_done": 2, "layer1_sum": 2,
    "weigh2_scaled": 4, "y_normed": 1, "var_eps": 3, "xa_done": 1, "ffn_done": 1, "chain": VECTOR_LINKS,
    "values_out": 2, "f1_biased": 2, "layer2_sum": 2, "rstd_done": 3, "result_done": 1,
    "pool_chain": 3,
    "result_left": 1,
}


def build(nc, x, gamma_in, Wq, Wk, Wv, gnn_w, gnn_b, lin_w, lin_b, Wo, gamma_out,
          Wg, Ws1, Ws3, Ws2, We1, We3, We2, out):
    B = x.shape[0]
    DM = x.shape[2]
    F = C * P
    FE = E * F
    assert x.shape[1] == T * P and DM == P

    with ExitStack() as ctx:
        def sb(name, shape, dt=F32):
            return ctx.enter_context(nc.sbuf_tensor(name, shape, dt))

        sem = {n: ctx.enter_context(nc.semaphore(n)) for n in PER_SEQ}
        once = {n: ctx.enter_context(nc.semaphore(n)) for n in (
            "ld_x0", "ld_x", "ld_q", "ld_v", "ld_g", "ld_o", "ld_e", "pool_setup", "setup_product", "act_setup", "dve_setup",
            "counters_set", "stored", "first_var_eps", "first_rstd", "first_xa", "dve_chain")}

        def need(eng, b, name, count):
            assert 0 <= count <= PER_SEQ[name], (name, count)
            eng.wait_ge(sem[name], b * PER_SEQ[name] + count + 1)

        psum = ctx.enter_context(nc.psum_tensor("psum", [P, BANKS, 512], F32))
        slot = {job: n for n, job in enumerate(JOBS)}

        def bank(kind, i):
            return psum[:, slot[kind, i] % BANKS, :]

        ident = sb("ident", [P, P])
        ones = sb("ones", [P, P])
        mask0 = sb("mask0", [P, P])
        mask1 = sb("mask1", [P, 2 * P])
        rank = sb("rank", [P, 8])
        minus_half = sb("minus_half", [P, T])
        gamma_col = sb("gamma_col", [P, 1])
        gamma_out_row = sb("gamma_out_row", [P, P])
        b1_row = sb("b1_row", [P, 2 * DH])
        b2_row = sb("b2_row", [P, DH])
        lin_b_col = sb("lin_b_col", [DH, 1])
        lin_sb = sb("lin_sb", [DH, DH])
        lin_t = sb("lin_t", [DH, DH])
        w1_2 = sb("w1_2", [P, P])
        w2_2 = sb("w2_2", [P, P])
        m_w = sb("m_w", [P, H, P])
        vh_w = sb("vh_w", [P, H, 2 * DH])
        o_w = sb("o_w", [P, H, P])
        out_bias = sb("out_bias", [P, 1])
        wg = sb("wg", [P, 8])
        w_gate = sb("w_gate", [P, E, F])
        w_up = sb("w_up", [P, E, F])
        w_down = sb("w_down", [P, E, C, P])

        x_all = sb("x_all", [P, B + 1, T, P])
        xn = sb("xn", [P, T, P])
        xa = sb("xa", [P, T, P])
        xa_t = sb("xa_t", [P, T * P])
        xn_t = sb("xn_t", [P, T * P])
        stats = sb("stats", [P, T, 6])
        mv = sb("mv", [P, T, 2])
        var_eps = sb("var_eps", [P, T])
        rstd = sb("rstd", [P, T])
        qm = sb("qm", [P, 2, 2, T * P])
        vh = sb("vh", [P, T, H, VHW])
        work = sb("work", [P, 8 * 3 * P])
        sm = work[:, 0:4 * 3 * P].rearrange("p (h n) -> p h n", h=4)
        mx = sb("mx", [P, H, T])
        negmax = sb("negmax", [P, H, T])
        ex = work[:, 4 * 3 * P:8 * 3 * P].rearrange("p (h k j) -> p h k j", h=4, k=3)
        D = sb("D", [P, H, T])
        et = sb("et", [P, H, 3 * P])
        spare = et[:].rearrange("p h n -> p (h n)")
        hd = H * DH
        wt = spare[:, 0:3 * hd].rearrange("p (k q d) -> p k q d", k=3, q=PAIRS)
        wq, wk, wv = (spare[:, n * hd:(n + 1) * hd] for n in (3, 4, 5))
        l1 = sb("l1", [P, H, T, VHW])
        rD = sb("rD", [P, H, T])
        rG = sb("rG", [P, H, T])
        kV = sb("kV", [P, H, T])
        h1 = sb("h1", [P, T, H, DH])
        h2 = h1
        f1 = sb("f1", [P, T, H, DH])
        f1b = sb("f1b", [P, T, H, DH])
        zt = work[:, 0:PAIRS * T * P].rearrange("p (q n) -> p q n", q=PAIRS)
        of = sb("of", [P, T, H, 2, DH])
        vo = sb("vo", [P, T, H // 2, DH])
        of_t = l1[:].rearrange("p h t d -> p (h t d)")[:, 0:H * T * P].rearrange("p (h n) -> p h n", h=H)
        y_t = sb("y_t", [P, T * P])
        yn = sb("yn", [P, T, P])
        th = sb("th", [P, 2, C * T * P])
        silu = sb("silu", [P, 2, C * T * P])
        hid = sb("hid", [P, 2, C, T * P])
        ffn = sb("ffn", [P, T, P])
        result = sb("result", [P, T, P])
        ez = sb("ez", [P, T, 8])
        gates = sb("gates_sb", [P, T, 8])
        gw = sb("gw", [P, 8, T, 8])
        gv = sb("gv", [P, 6, T])
        w_exp = sb("w_exp", [P, T, 8])
        carrier = sb("carrier", [P, 48])

        x_dram = x.rearrange("b (t p) d -> p b t d", p=P)
        out_dram = out.rearrange("b (t p) d -> b p t d", p=P)

        block = ctx.enter_context(nc.Block())

        def bc(ap, n):
            return ap.unsqueeze(len(ap.shape)).to_broadcast(list(ap.shape) + [n])

        def heads_t(ap):
            return ap.rearrange("p h t -> p t h")

        LOADS = dict(ld_x0=1, ld_x=1, ld_q=2, ld_v=6, ld_g=3, ld_o=3, ld_e=8)

        def loaded(eng, name):
            eng.wait_ge(once[name], 16 * LOADS[name])

        @block.sync
        def _(sp):
            sp.dma_start(x_all[:, 0, :, :], x_dram[:, 0]).then_inc(once["ld_x0"], 16)
            sp.dma_start(wq, Wq).then_inc(once["ld_q"], 16)
            sp.dma_start(wv, Wv).then_inc(once["ld_v"], 16)
            sp.wait_ge(once["pool_setup"], 3)
            for n in range(2):
                for k, w in ((0, w1_2), (1, w2_2)):
                    sp.dma_start(w[n * DH:(n + 1) * DH, n * DH:(n + 1) * DH], gnn_w[k]).then_inc(once["ld_v"], 16)
            sp.dma_start(b1_row[:, DH:2 * DH], gnn_b[0].partition_broadcast(P)).then_inc(once["ld_v"], 16)
            sp.dma_start(x_all[:, 1:B], x_dram[:, 1:B]).then_inc(once["ld_x"], 16)
            sp.dma_start(w_gate[:, 0, :], Ws1).then_inc(once["ld_e"], 16)
            sp.dma_start(w_up[:, 0, :], Ws3).then_inc(once["ld_e"], 16)
            sp.dma_start(w_down[:, 0], Ws2.rearrange("(c p) d -> p c d", p=P)).then_inc(once["ld_e"], 16)
            sp.dma_start(w_down[:, 1:5], We2[0:4].rearrange("e (c p) d -> p e c d", p=P)).then_inc(once["ld_e"], 16)
            sp.dma_start(w_down[:, 5:9], We2[4:8].rearrange("e (c p) d -> p e c d", p=P)).then_inc(once["ld_e"], 16)
            for n in sem:
                sp.sem_inc(sem[n], 1)
            sp.sem_inc(once["counters_set"], 1)
            with sp.Fori(0, B) as b:
                need(sp, b, "result_done", 1)
                sp.dma_start(out_dram[b], result[:]).then_inc(once["stored"], 16)
                sp.wait_ge(once["stored"], b * 16 + 16)
                sp.sem_inc(sem["result_left"], 1)
            sp.wait_ge(once["stored"], 16 * B)

        SETUP = (["x_turn"] + ["w_turn"] * 6 + ["m"] * 4 + ["vw1"] * 2 + ["lin_turn"] + ["lin_wo"] * 4 + ["bias"])
        first = {k: SETUP.index(k) for k in SETUP}

        def emptied(eng, n):
            eng.wait_ge(once["dve_setup" if n % 2 == 0 else "act_setup"], n // 2 + 1)

        def all_emptied(eng, upto):
            emptied(eng, upto)
            if upto >= 1:
                emptied(eng, upto - 1)

        def empty_setup(eng, copy, parity, name):
            for n in range(parity, len(SETUP), 2):
                src = psum[:, n % BANKS, :]
                kind, k = SETUP[n], n - first[SETUP[n]]
                eng.wait_ge(once["setup_product"], n + 1)
                if kind == "x_turn":
                    copy(xa_t[:], src[:, 0:T * P], gamma_col[:, 0:1])
                    ins = copy(xn_t[:], src[:, T * P:2 * T * P], 1.0)
                elif kind == "w_turn":
                    ins = copy(wt.rearrange("p k q d -> p (k q) d")[:, 4 * k:4 * k + 4, :],
                               src.rearrange("p (q d) -> p q d", q=4), 1.0)
                elif kind == "m":
                    ins = copy(m_w[:, 8 * (k // 2) + k % 2:8 * (k // 2) + 8:2, :], src.rearrange("p (q d) -> p q d", q=4), DH ** -0.5)
                elif kind == "vw1":
                    ins = copy(vh_w[:, 8 * k:8 * k + 8, DH:2 * DH], src.rearrange("p (q d) -> p q d", q=8), 1.0)
                elif kind == "lin_turn":
                    ins = copy(lin_t[:], src[0:DH, 0:DH], 1.0)
                elif kind == "lin_wo":
                    ins = copy(o_w[DH:P, 4 * k:4 * k + 4, :],
                               src[DH:P, :].rearrange("p (q d) -> p q d", q=4), 1.0)
                else:
                    ins = copy(out_bias[:], src[:, 0:1], 1.0)
                ins.then_inc(once[name], 1)

        @block.gpsimd
        def _(pool):
            pool.memset(w1_2[:], 0.0).then_inc(once["pool_setup"], 1)
            pool.memset(w2_2[:], 0.0).then_inc(once["pool_setup"], 1)
            pool.memset(b1_row[:], 0.0).then_inc(once["pool_setup"], 1)
            pool.memset(x_all[:, B], 0.0)
            pool.memset(minus_half[:], -0.5)
            pool.memset(mask0[:], 0.0)
            pool.memset(mask1[:], 0.0)
            pool.memset(vh[:, :, :, 2 * DH:VHW], 1.0)
            pool.memset(ones[:], 1.0).then_inc(once["pool_setup"], 1)
            pool.iota(rank[:], pattern=[[-1, 8]], base=8, channel_multiplier=0,
                      allow_small_or_imprecise_dtypes=True)
            pool.wait_ge(once["pool_setup"], 4)
            pool.affine_select(out=ident[:], in_=ones[:], compare_op=ALU.is_equal, fill=0.0, base=0,
                               pattern=[[-1, P]], channel_multiplier=1)
            pool.affine_select(out=mask0[:], in_=mask0[:], compare_op=ALU.is_ge, fill=MASKED, base=0,
                               pattern=[[-1, P]], channel_multiplier=1)
            pool.affine_select(out=mask1[:, P:2 * P], in_=mask1[:, P:2 * P], compare_op=ALU.is_ge,
                               fill=MASKED, base=0, pattern=[[-1, P]],
                               channel_multiplier=1).then_inc(once["pool_setup"], 1)
            for n in range(2):
                pool.wait_ge(once["first_var_eps"], n + 1)
                pool.tensor_tensor(rstd[:], var_eps[:], minus_half[:], ALU.pow).then_inc(once["first_rstd"], 1)
            loaded(pool, "ld_v")
            pool.tensor_copy(vh_w[:, :, 0:DH], wv.rearrange("p (h d) -> p h d", h=H)).then_inc(once["pool_setup"], 1)
            loaded(pool, "ld_g")

            def rstd_of(b, n):
                need(pool, b, "var_eps", n + 1)
                pool.tensor_tensor(rstd[:], var_eps[:], minus_half[:], ALU.pow).then_inc(sem["rstd_done"], 1)

            pool.wait_ge(once["counters_set"], 1)
            with pool.Fori(0, B) as b:
                for hf in range(2):
                    hs = slice(hf * PAIRS, (hf + 1) * PAIRS)
                    need(pool, b, "norms_done", hf + 1)
                    need(pool, b, "stack", 0)
                    if hf == 1:
                        need(pool, b, "values_out", 1)
                    pool.tensor_tensor(vo[:], vh[:, :, hs, 0:DH], bc(heads_t(kV[:, hs]), DH), ALU.mult)
                    pool.tensor_tensor(of[:, :, hs, 0, :], l1[:, hs, :, 0:DH].rearrange("p h t d -> p t h d"),
                                       bc(heads_t(rD[:, hs]), DH), ALU.mult).then_inc(sem["pool_chain"], 1)
                    need(pool, b, "pool_chain", hf + 1)
                    pool.tensor_tensor(of[:, :, hs, 0, :], of[:, :, hs, 0, :], vo[:],
                                       ALU.add).then_inc(sem["values_out"], 1)
                for hf in range(2):
                    hs = slice(hf * PAIRS, (hf + 1) * PAIRS)
                    need(pool, b, "gelu1_done", hf + 1)
                    pool.tensor_tensor(f1b[:, :, hs, :], f1[:, :, hs, :],
                                       b2_row[:].unsqueeze(1).unsqueeze(1).to_broadcast([P, T, PAIRS, DH]),
                                       ALU.add).then_inc(sem["f1_biased"], 1)
                rstd_of(b, 0)
                rstd_of(b, 1)
                for hf in range(2):
                    hs = slice(hf * PAIRS, (hf + 1) * PAIRS)
                    need(pool, b, "weigh2_scaled", 2 * hf + 2)
                    need(pool, b, "f1_biased", hf + 1)
                    pool.tensor_tensor(h2[:, :, hs, :], h2[:, :, hs, :], f1b[:, :, hs, :],
                                       ALU.add).then_inc(sem["layer2_sum"], 1)
                rstd_of(b, 2)
                need(pool, b, "ffn_done", 1)
                need(pool, b, "y_normed", 1)
                pool.tensor_tensor(yn[:], yn[:], gamma_out_row[:].unsqueeze(1).to_broadcast([P, T, P]),
                                   ALU.mult).then_inc(sem["pool_chain"], 1)
                need(pool, b, "pool_chain", 3)
                need(pool, b, "result_left", 0)
                pool.tensor_tensor(result[:], yn[:], ffn[:], ALU.add).then_inc(sem["result_done"], 1)

        @block.scalar
        def _(act):
            act.dma_start(gamma_col[:], gamma_in.rearrange("(p o) -> p o", o=1)).then_inc(once["ld_g"], 16)
            act.dma_start(wk, Wk).then_inc(once["ld_q"], 16)
            act.dma_start(o_w[0:DH], Wo.rearrange("(h p) n -> p h n", p=DH)).then_inc(once["ld_o"], 16)
            act.dma_start(lin_sb[:], lin_w).then_inc(once["ld_o"], 16)
            act.dma_start(lin_b_col[:], lin_b.rearrange("(p o) -> p o", o=1)).then_inc(once["ld_o"], 16)
            act.dma_start(b2_row[:], gnn_b[1].partition_broadcast(P)).then_inc(once["ld_g"], 16)
            act.dma_start(gamma_out_row[:], gamma_out.partition_broadcast(P)).then_inc(once["ld_g"], 16)
            act.dma_start(wg[:], Wg).then_inc(once["ld_e"], 16)
            act.dma_start(w_gate[:, 1:E, :], We1.rearrange("e d f -> d e f")).then_inc(once["ld_e"], 16)
            act.dma_start(w_up[:, 1:E, :], We3.rearrange("e d f -> d e f")).then_inc(once["ld_e"], 16)
            empty_setup(act, lambda o, i, s: nc.scalar.activation(o, i, ACT.Copy, scale=s), 1, "act_setup")
            all_emptied(act, len(SETUP) - 1)

            def read(b, kind, n):
                need(act, b, kind, n + 1)
                return bank(kind, n)

            def copy_qm(b, p):
                src = read(b, "qm", p)
                if p >= 2:
                    need(act, b, "scores", 2 * p - 2)
                nc.scalar.copy(qm[:, p % 2].rearrange("p a n -> p (a n)"), src).then_inc(sem["qm_copied"], 1)

            def exps(b, h):
                need(act, b, "negmax_done", h // 2 + 1)
                if h >= 4:
                    need(act, b, "turn", h - 3)
                for t in range(T):
                    blocks = slice(0, 1) if t == 0 else slice(1, 3)
                    cols = slice(0, P) if t == 0 else slice(P, 3 * P)
                    nc.scalar.activation(ex[:, h % 4, blocks, :].rearrange("p k j -> p (k j)"), sm[:, h % 4, cols],
                                         ACT.Exp, bias=negmax[:, h, t:t + 1], scale=1.0,
                                         accum_out=D[:, h, t:t + 1]).then_inc(sem["exp_done"], 1)

            def copy_et(b, h):
                src = read(b, "turn", h)
                nc.scalar.copy(et[:, h, :], src[:, 0:3 * P]).then_inc(sem["et_copied"], 1)

            def copy_l1(b, h):
                src = read(b, "layer1", h)
                nc.scalar.copy(l1[:, h, :, :], src[:, 0:T * VHW].rearrange("p (t d) -> p t d", t=T)
                               ).then_inc(sem["layer1_copied"], 1)

            def tanh(b, e):
                src = read(b, "gate_up", e)
                if e >= 2:
                    need(act, b, "silu_made", e - 1)
                nc.scalar.activation(th[:, e % 2, :], src, ACT.Tanh, scale=0.5).then_inc(sem["tanh_done"], 1)

            def gelu1(b, hf):
                hs = slice(hf * PAIRS, (hf + 1) * PAIRS)
                need(act, b, "layer1_sum", hf + 1)
                nc.scalar.activation(f1[:, :, hs, :], h1[:, :, hs, :], ACT.Gelu).then_inc(sem["gelu1_done"], 1)

            def gelu2(b, hf):
                hs = slice(hf * PAIRS, (hf + 1) * PAIRS)
                need(act, b, "layer2_sum", hf + 1)
                nc.scalar.activation(of[:, :, hs, 1, :], h2[:, :, hs, :], ACT.Gelu).then_inc(sem["gelu2_done"], 1)

            def copy_z(b, g):
                src = read(b, "layer2", g)
                nc.scalar.copy(zt[:, 2 * g:2 * g + 2, :].rearrange("p q n -> p (q n)"), src
                               ).then_inc(sem["z_copied"], 1)

            def copy_stack(b, p):
                src = read(b, "stack", p)
                nc.scalar.copy(of_t[:, 2 * p:2 * p + 2, :].rearrange("p q n -> p (q n)"), src
                               ).then_inc(sem["stack_copied"], 1)

            act.wait_ge(once["counters_set"], 1)
            with act.Fori(0, B) as b:
                src = read(b, "gates", 0)
                need(act, b, "chain", 0)
                nc.scalar.activation(ez[:], src[:, 0:T * 8].rearrange("p (t e) -> p t e", t=T), ACT.Exp,
                                     scale=-1.0).then_inc(sem["gates_taken"], 1)
                copy_qm(b, 0)
                need(act, b, "norms_done", 0)
                need(act, b, "values_out", 0)
                need(act, b, "layer1_sum", 0)
                for s in range(PAIRS):
                    exps(b, 2 * s)
                    if s + 1 < PAIRS:
                        copy_qm(b, s + 1)
                    exps(b, 2 * s + 1)
                    if s >= 1:
                        copy_et(b, 2 * s - 2)
                        copy_et(b, 2 * s - 1)
                    if s >= 2:
                        copy_l1(b, 2 * s - 4)
                        copy_l1(b, 2 * s - 3)
                tanh(b, 0)
                for h in (H - 2, H - 1):
                    copy_et(b, h)
                for h in (H - 4, H - 3):
                    copy_l1(b, h)
                tanh(b, 1)
                for h in (H - 2, H - 1):
                    copy_l1(b, h)
                gelu1(b, 0)
                tanh(b, 2)
                tanh(b, 3)
                gelu1(b, 1)
                tanh(b, 4)
                tanh(b, 5)
                copy_z(b, 0)
                copy_z(b, 1)
                tanh(b, 6)
                copy_z(b, 2)
                copy_z(b, 3)
                tanh(b, 7)
                gelu2(b, 0)
                tanh(b, 8)
                copy_stack(b, 0)
                copy_stack(b, 1)
                gelu2(b, 1)
                copy_stack(b, 2)
                copy_stack(b, 3)
                src = read(b, "x_turn", 0)
                nc.scalar.activation(xa_t[:], src[:, 0:T * P], ACT.Copy, scale=gamma_col[:, 0:1]
                                     ).then_inc(sem["xt_copied"], 1)
                nc.scalar.copy(xn_t[:], src[:, T * P:2 * T * P]).then_inc(sem["xt_copied"], 1)
                for p in range(4, 8):
                    copy_stack(b, p)
                src = read(b, "out", 0)
                nc.scalar.activation(y_t[:], src[:, 0:T * P], ACT.Identity, bias=out_bias[:, 0:1]
                                     ).then_inc(sem["y_copied"], 1)

        @block.vector
        def _(dve):
            V = nc.vector

            carried = [0]

            def carry_wait():
                carried[0] += 1
                V.memset(carrier[:, carried[0] - 1:carried[0]], 0.0)

            def mean_var(n, src, link):
                for t in range(T):
                    ins = V.bn_stats(stats[:, t, :], src(t))
                link(ins)
                carry_wait()
                for t in range(T):
                    ins = V.bn_aggr(mv[:, t, :], stats[:, t, :])
                link(ins)
                return V.tensor_scalar(var_eps[:], mv[:, :, 1], EPS, None, ALU.add)

            def normed(dst, src):
                for t in range(T):
                    ins = V.tensor_scalar(dst(t), src(t), mv[:, t, 0:1], rstd[:, t:t + 1], ALU.subtract, ALU.mult)
                return ins

            links = [0]

            def link_once(ins):
                links[0] += 1
                ins.then_inc(once["dve_chain"], 1)
                dve.wait_ge(once["dve_chain"], links[0])

            loaded(dve, "ld_x0")
            mean_var(0, lambda t: x_all[:, 0, t, :], link_once).then_inc(once["first_var_eps"], 1)
            dve.wait_ge(once["first_rstd"], 1)
            link_once(normed(lambda t: xn[:, t, :], lambda t: x_all[:, 0, t, :]))
            mean_var(1, lambda t: xn[:, t, :], link_once).then_inc(once["first_var_eps"], 1)
            dve.wait_ge(once["first_rstd"], 2)
            normed(lambda t: xa[:, t, :], lambda t: xn[:, t, :]).then_inc(once["first_xa"], 1)
            loaded(dve, "ld_g")
            loaded(dve, "ld_x")
            loaded(dve, "ld_v")
            dve.wait_ge(once["pool_setup"], 6)
            empty_setup(dve, lambda o, i, s: V.tensor_scalar(o, i, s, None, ALU.mult), 0, "dve_setup")
            all_emptied(dve, len(SETUP) - 1)

            def read(b, kind, n):
                need(dve, b, kind, n + 1)
                return bank(kind, n)

            def mask_scores(b, p):
                for h in (2 * p, 2 * p + 1):
                    src = read(b, "scores", h)
                    if h >= 4:
                        need(dve, b, "exp_done", 2 * (h - 3))
                    carry_wait()
                    V.tensor_tensor_reduce(sm[:, h % 4, 0:P], src[:, 0:P], mask0[:], 1.0, MASKED,
                                           ALU.add, ALU.max, mx[:, h, 0:1])
                    V.tensor_tensor_reduce(sm[:, h % 4, P:3 * P], src[:, P:3 * P], mask1[:], 1.0, MASKED,
                                           ALU.add, ALU.max, mx[:, h, 1:2]).then_inc(sem["scores_masked"], 1)
                need(dve, b, "scores_masked", 2 * p + 2)
                V.tensor_scalar(negmax[:, 2 * p:2 * p + 2, :], mx[:, 2 * p:2 * p + 2, :], -1.0, None,
                                ALU.mult).then_inc(sem["negmax_done"], 1)

            def copy_vh(b, n):
                q, t = n // 2, n % 2
                src = read(b, "vh", n)
                V.tensor_tensor(vh[:, t, 4 * q:4 * q + 4, 0:2 * DH], src.rearrange("p (h d) -> p h d", h=4),
                                b1_row[:].unsqueeze(1).to_broadcast([P, 4, 2 * DH]),
                                ALU.add).then_inc(sem["vh_copied"], 1)

            def set_diagonal(b, p):
                need(dve, b, "exp_done", 4 * p + 4)
                carry_wait()
                r = 2 * (p % 2)
                V.copy_predicated(ex[:, r:r + 2, 0:3:2, :],
                                  ident[:].bitcast(U32).unsqueeze(1).unsqueeze(1).to_broadcast([P, 2, 2, P]),
                                  bc(D[:, 2 * p:2 * p + 2, :], P)).then_inc(sem["diag_set"], 1)

            def norms(b, hf, link):
                hs = slice(hf * PAIRS, (hf + 1) * PAIRS)
                need(dve, b, "layer1_copied", PAIRS * (hf + 1))
                V.reciprocal(rG[:, hs], l1[:, hs, :, 2 * DH])
                link(V.reciprocal(rD[:, hs], D[:, hs]))
                link(V.tensor_tensor(kV[:, hs], l1[:, hs, :, 2 * DH], rD[:, hs], ALU.mult))
                V.tensor_scalar(kV[:, hs], kV[:, hs], -1.0, 1.0, ALU.mult, ALU.add).then_inc(sem["norms_done"], 1)
                if hf == 0:
                    need(dve, b, "gelu2_done", 0)
                link(V.tensor_tensor(h1[:, :, hs, :], l1[:, hs, :, DH:2 * DH].rearrange("p h t d -> p t h d"),
                                     bc(heads_t(rG[:, hs]), DH), ALU.mult))
                V.tensor_tensor(h1[:, :, hs, :], h1[:, :, hs, :], vh[:, :, hs, 0:DH],
                                ALU.add).then_inc(sem["layer1_sum"], 1)

            def choose(b, link):
                need(dve, b, "gates_taken", 1)
                g, m, s1, o1, g2, s2, o2 = (gw[:, i] for i in range(7))
                v1, v2, p1, p2, den, rden = (gv[:, i] for i in range(6))
                ranks = rank[:].unsqueeze(1).to_broadcast([P, T, 8])
                link(V.tensor_scalar(g, ez[:], 1.0, None, ALU.add))
                link(V.reciprocal(gates[:], g))
                link(V.tensor_reduce(v1, gates[:], AX_X, ALU.max))
                link(V.tensor_tensor(m, gates[:], bc(v1, 8), ALU.is_equal))
                link(V.tensor_tensor(s1, m, ranks, ALU.mult))
                link(V.tensor_reduce(p1, s1, AX_X, ALU.max))
                link(V.tensor_tensor(o1, s1, bc(p1, 8), ALU.is_equal))
                link(V.scalar_tensor_tensor(out=g2, in0=o1, scalar=-4.0, in1=gates[:], op0=ALU.mult, op1=ALU.add))
                link(V.tensor_reduce(v2, g2, AX_X, ALU.max))
                link(V.tensor_tensor(m, g2, bc(v2, 8), ALU.is_equal))
                link(V.tensor_tensor(s2, m, ranks, ALU.mult))
                link(V.tensor_reduce(p2, s2, AX_X, ALU.max))
                link(V.tensor_tensor(o2, s2, bc(p2, 8), ALU.is_equal))
                V.tensor_tensor(den, v1, v2, ALU.add)
                link(V.tensor_tensor(m, o1, o2, ALU.add))
                V.reciprocal(rden, den)
                link(V.tensor_tensor(s2, m, gates[:], ALU.mult))
                link(V.tensor_tensor(s1, s2, bc(rden, 8), ALU.mult))
                link(V.tensor_scalar(w_exp[:], s1, 0.5 / 3.0, None, ALU.mult))

            def hidden(b, e):
                g = bank("gate_up", e)
                need(dve, b, "tanh_done", e + 1)
                if e >= 2:
                    need(dve, b, "down", e - 1)
                V.scalar_tensor_tensor(out=silu[:, e % 2, :], in0=th[:, e % 2, :], scalar=1.0, in1=g,
                                       op0=ALU.add, op1=ALU.mult).then_inc(sem["silu_made"], 1)
                u = read(b, "up", e)
                need(dve, b, "silu_made", e + 1)
                V.tensor_tensor(hid[:, e % 2].rearrange("p c n -> p (c n)"), silu[:, e % 2, :], u,
                                ALU.mult).then_inc(sem["hidden_made"], 1)

            def add_down(b, e):
                src = read(b, "down", e)
                if e == 0:
                    need(dve, b, "result_done", 0)
                    V.tensor_scalar(ffn[:], src[:, 0:T * P].rearrange("p (t d) -> p t d", t=T), 0.5 / 3.0, None,
                                    ALU.mult).then_inc(sem["down_added"], 1)
                    return
                need(dve, b, "down_added", e)
                for t in range(T):
                    ins = V.scalar_tensor_tensor(out=ffn[:, t, :], in0=src[:, t * P:(t + 1) * P],
                                                 scalar=w_exp[:, t, e - 1:e], in1=ffn[:, t, :],
                                                 op0=ALU.mult, op1=ALU.add)
                ins.then_inc(sem["down_added"], 1)

            def scale_weigh2(b, n):
                q, t = n // 2, n % 2
                hs = slice(q * PAIRS, (q + 1) * PAIRS)
                src = read(b, "weigh2", n)
                V.tensor_tensor(h2[:, t, hs, :], src.rearrange("p (h d) -> p h d", h=PAIRS),
                                bc(rG[:, hs, t], DH), ALU.mult).then_inc(sem["weigh2_scaled"], 1)

            dve.wait_ge(once["counters_set"], 1)
            with dve.Fori(0, B) as b:
                count = [0]

                def link(ins):
                    count[0] += 1
                    ins.then_inc(sem["chain"], 1)
                    need(dve, b, "chain", count[0])

                for p in range(PAIRS):
                    mask_scores(b, p)
                    copy_vh(b, p)
                    set_diagonal(b, p)
                norms(b, 0, link)
                hidden(b, 0)
                choose(b, link)
                hidden(b, 1)
                norms(b, 1, link)
                hidden(b, 2)
                add_down(b, 0)
                need(dve, b, "x_turn", 0)
                mean_var(0, lambda t: x_all[:, b + 1, t, :], link).then_inc(sem["var_eps"], 1)
                hidden(b, 3)
                add_down(b, 1)
                need(dve, b, "rstd_done", 1)
                link(normed(lambda t: xn[:, t, :], lambda t: x_all[:, b + 1, t, :]))
                mean_var(1, lambda t: xn[:, t, :], link).then_inc(sem["var_eps"], 1)
                hidden(b, 4)
                add_down(b, 2)
                need(dve, b, "rstd_done", 2)
                normed(lambda t: xa[:, t, :], lambda t: xn[:, t, :]).then_inc(sem["xa_done"], 1)
                hidden(b, 5)
                add_down(b, 3)
                hidden(b, 6)
                scale_weigh2(b, 0)
                scale_weigh2(b, 1)
                add_down(b, 4)
                hidden(b, 7)
                scale_weigh2(b, 2)
                scale_weigh2(b, 3)
                add_down(b, 5)
                hidden(b, 8)
                for e in (6, 7, 8):
                    add_down(b, e)
                need(dve, b, "down_added", E)
                V.tensor_tensor(ffn[:], ffn[:], x_all[:, b], ALU.add).then_inc(sem["ffn_done"], 1)
                y = read(b, "out_turn", 0)
                mean_var(2, lambda t: y[:, t * P:(t + 1) * P], link).then_inc(sem["var_eps"], 1)
                need(dve, b, "rstd_done", 3)
                normed(lambda t: yn[:, t, :], lambda t: y[:, t * P:(t + 1) * P]).then_inc(sem["y_normed"], 1)
                assert count[0] == VECTOR_LINKS, count[0]

        @block.tensor
        def _(pe):
            def setup_bank(n):
                if n >= BANKS:
                    emptied(pe, n - BANKS)
                return psum[:, n % BANKS, :]

            pe.wait_ge(once["pool_setup"], 5)
            pe.wait_ge(once["first_xa"], 1)
            for n, kind in enumerate(SETUP):
                k = n - first[kind]
                dst = setup_bank(n)
                if kind == "x_turn":
                    for j, src in enumerate((xa, xn)):
                        for t in range(T):
                            ins = pe.transpose(dst[:, (2 * j + t) * P:(2 * j + t + 1) * P], src[:, t, :], ident[:])
                elif kind == "w_turn":
                    if k == 0:
                        loaded(pe, "ld_q")
                    if k == 4:
                        loaded(pe, "ld_v")
                    w = (wq, wk, wv)[k // 2]
                    for j in range(4):
                        p = 4 * (k % 2) + j
                        ins = pe.transpose(dst[:, j * P:(j + 1) * P], w[:, p * P:(p + 1) * P], ident[:])
                elif kind == "m":
                    if k == 0:
                        all_emptied(pe, first["w_turn"] + 3)
                    for j in range(4):
                        h = 8 * (k // 2) + 2 * j + k % 2
                        rows = slice(DH * (h % 2), DH * (h % 2) + DH)
                        ins = pe.matmul(dst[:, j * P:(j + 1) * P], wt[rows, 0, h // 2, :], wt[rows, 1, h // 2, :],
                                        start=True, stop=True)
                elif kind == "vw1":
                    if k == 0:
                        all_emptied(pe, first["w_turn"] + 5)
                    for j in range(4):
                        ins = pe.matmul(dst[:, j * P:(j + 1) * P], wt[:, 2, 4 * k + j, :], w1_2[:],
                                        start=True, stop=True)
                elif kind == "lin_turn":
                    loaded(pe, "ld_o")
                    ins = pe.transpose(dst[0:DH, 0:DH], lin_sb[:], ident[0:DH, 0:DH])
                elif kind == "lin_wo":
                    if k == 0:
                        emptied(pe, first["lin_turn"])
                    ins = pe.matmul(dst[DH:P, :], lin_t[:],
                                    o_w[0:DH, 4 * k:4 * k + 4, :].rearrange("p h n -> p (h n)"),
                                    start=True, stop=True)
                else:
                    for h in range(H):
                        ins = pe.matmul(dst[:, 0:1], o_w[0:DH, h, :], lin_b_col[:], start=h == 0, stop=h == H - 1)
                ins.then_inc(once["setup_product"], 1)
            all_emptied(pe, len(SETUP) - 1)
            loaded(pe, "ld_e")
            pe.wait_ge(once["pool_setup"], 6)

            done_e = [False]

            def free_bank(b, n):
                if n >= BANKS:
                    kind, i = JOBS[n - BANKS]
                    need(pe, b, READ_BY[kind], i * (2 if kind == "x_turn" else 1) + (2 if kind == "x_turn" else 1))
                elif SLOTS - BANKS + n < len(JOBS):
                    need(pe, b, READ_BY[JOBS[SLOTS - BANKS + n][0]], 0)

            def product(b, kind, i):
                dst = bank(kind, i)
                if kind == "gates":
                    for t in range(T):
                        ins = pe.matmul(dst[:, t * 8:t * 8 + 8], xn_t[:, t * P:(t + 1) * P], wg[:],
                                        start=True, stop=True)
                elif kind == "qm":
                    for j in range(2):
                        ins = pe.matmul(dst[:, j * T * P:(j + 1) * T * P], m_w[:, 2 * i + j, :], xa_t[:],
                                        start=True, stop=True)
                elif kind == "scores":
                    need(pe, b, "qm_copied", i // 2 + 1)
                    q = qm[:, (i // 2) % 2, i % 2, :]
                    pe.matmul(dst[:, 0:P], q[:, 0:P], xa_t[:, 0:P], start=True, stop=True)
                    ins = pe.matmul(dst[:, P:3 * P], q[:, P:2 * P], xa_t[:], start=True, stop=True)
                elif kind == "vh":
                    q, t = i // 2, i % 2
                    ins = pe.matmul(dst, xa_t[:, t * P:(t + 1) * P],
                                    vh_w[:, 4 * q:4 * q + 4, :].rearrange("p h d -> p (h d)"),
                                    start=True, stop=True)
                elif kind == "turn":
                    need(pe, b, "diag_set", i // 2 + 1)
                    for k in range(3):
                        ins = pe.transpose(dst[:, k * P:(k + 1) * P], ex[:, i % 4, k, :], ident[:])
                elif kind == "layer1":
                    need(pe, b, "et_copied", i + 1)
                    need(pe, b, "vh_copied", 2 * (i // 4) + 2)
                    pe.matmul(dst[:, 0:VHW], et[:, i, 0:P], vh[:, 0, i, :], start=True, stop=True)
                    pe.matmul(dst[:, VHW:2 * VHW], et[:, i, P:2 * P], vh[:, 0, i, :], start=True, stop=False)
                    ins = pe.matmul(dst[:, VHW:2 * VHW], et[:, i, 2 * P:3 * P], vh[:, 1, i, :],
                                    start=False, stop=True)
                elif kind in ("gate_up", "up"):
                    w = w_gate if kind == "gate_up" else w_up
                    for c in range(C):
                        ins = pe.matmul(dst[:, c * T * P:(c + 1) * T * P], w[:, i, c * P:(c + 1) * P], xn_t[:],
                                        start=True, stop=True)
                elif kind == "down":
                    need(pe, b, "hidden_made", i + 1)
                    for t in range(T):
                        for c in range(C):
                            ins = pe.matmul(dst[:, t * P:(t + 1) * P], hid[:, i % 2, c, t * P:(t + 1) * P],
                                            w_down[:, i, c, :], start=c == 0, stop=c == C - 1)
                elif kind == "layer2":
                    need(pe, b, "gelu1_done", i // 2 + 1)
                    for j in range(2):
                        for r in range(2):
                            h = 4 * i + 2 * j + r
                            rows = slice(DH * r, DH * r + DH)
                            at = j * T * P
                            pe.matmul(dst[rows, at:at + T * P], f1[:, 0, h, :], et[:, h, 0:2 * P],
                                      start=True, stop=False)
                            ins = pe.matmul(dst[rows, at + P:at + 2 * P], f1[:, 1, h, :], et[:, h, 2 * P:3 * P],
                                            start=False, stop=True)
                elif kind == "weigh2":
                    q, t = i // 2, i % 2
                    need(pe, b, "z_copied", 2 * q + 2)
                    for j in range(4):
                        ins = pe.matmul(dst[:, j * P:(j + 1) * P], zt[:, 4 * q + j, t * P:(t + 1) * P], w2_2[:],
                                        start=True, stop=True)
                elif kind == "stack":
                    need(pe, b, "gelu2_done", i // 4 + 1)
                    need(pe, b, "values_out", i // 4 + 1)
                    for j in range(2):
                        for t in range(T):
                            ins = pe.transpose(dst[:, (2 * j + t) * P:(2 * j + t + 1) * P],
                                               of[:, t, 2 * i + j].rearrange("p k d -> p (k d)"), ident[:])
                elif kind == "x_turn":
                    need(pe, b, "xa_done", 1)
                    for j, src in enumerate((xa, xn)):
                        for t in range(T):
                            ins = pe.transpose(dst[:, (2 * j + t) * P:(2 * j + t + 1) * P], src[:, t, :], ident[:])
                elif kind == "out":
                    for h in range(H):
                        if h % 2 == 0:
                            need(pe, b, "stack_copied", h // 2 + 1)
                        ins = pe.matmul(dst[:, 0:T * P], o_w[:, h, :], of_t[:, h, :], start=h == 0, stop=h == H - 1)
                elif kind == "out_turn":
                    need(pe, b, "y_copied", 1)
                    for t in range(T):
                        ins = pe.transpose(dst[:, t * P:(t + 1) * P], y_t[:, t * P:(t + 1) * P], ident[:])
                return ins

            pe.wait_ge(once["counters_set"], 1)
            with pe.Fori(0, B) as b:
                need(pe, b, "xt_copied", 0)
                for n, (kind, i) in enumerate(JOBS):
                    free_bank(b, n)
                    product(b, kind, i).then_inc(sem[kind], 1)


_INS = ["x", "gamma_in", "Wq", "Wk", "Wv", "gnn_w", "gnn_b", "lin_w", "lin_b", "Wo", "gamma_out"]
_FFN = ["Wg", "Ws1", "Ws3", "Ws2", "We1", "We3", "We2"]


def kernel(**inputs):
    import numpy as np
    import concourse.bacc as bacc
    from concourse.bass_utils import run_bass_kernel_spmd

    nc = bacc.Bacc("TRN2", target_bir_lowering=False, num_devices=1)
    arrays, args = {}, []
    for name in ["L0_attn_" + n for n in _INS] + ["L0_ffn_" + n for n in _FFN]:
        a = np.ascontiguousarray(inputs[name])
        arrays[f"in_{name}"] = a
        args.append(nc.dram_tensor(f"in_{name}", a.shape, mybir.dt.from_np(a.dtype), kind="ExternalInput").ap())
    out = nc.dram_tensor("out", inputs["L0_attn_x"].shape, F32, kind="ExternalOutput").ap()
    build(nc, *args, out)
    r = run_bass_kernel_spmd(nc, [arrays], core_ids=[0])
    return r.results[0]["out"]
```

```python
from contextlib import ExitStack

import concourse.bass as bass
from concourse import mybir
from concourse.alu_op_type import AluOpType as ALU

F32 = mybir.dt.float32
F32R = mybir.dt.float32r
U32 = mybir.dt.uint32
ACT = mybir.ActivationFunctionType
AX_X = mybir.AxisListType.X

P = 128
T = 2
H, DH = 16, 64
PAIRS = H // 2
E = 9
C = 2
VHW = 2 * DH + 2
BANKS = 8
STACKS = 2
EPS = 1e-5
MASKED = -3.0e38


def product_jobs():
    jobs = []
    up = lambda e: [("gate_up", e), ("up", e)]
    two = lambda kind, n: [(kind, 2 * n), (kind, 2 * n + 1)]
    for s in range(PAIRS):
        if s >= 1:
            jobs += two("turn", s - 1)
        if s + 1 < PAIRS:
            jobs += two("scores", s + 1)
        jobs.append(("vh", s))
        if s + 2 < PAIRS:
            jobs.append(("qm", s + 2))
        if s >= 2:
            jobs += up(s - 2)
        if s >= 1:
            jobs += two("layer1", s - 1)
        if s >= 3:
            jobs.append(("down", s - 3))
    jobs += two("turn", PAIRS - 1) + up(6) + two("layer1", PAIRS - 1) + [("down", 5)]
    jobs += two("layer2", 0) + up(7) + two("weigh2", 0) + [("down", 6)]
    jobs += two("layer2", 1) + up(8) + [("x_turn", 0), ("down", 7)] + two("weigh2", 1)
    stack = lambda p: ("stack", p)
    part = lambda p: ("out", p)
    jobs += [("gates", 1), ("qm", PAIRS), stack(0), ("qm", PAIRS + 1), stack(1), ("down", 8), stack(2), part(0), part(1)]
    jobs += [stack(3), part(2), stack(4), part(3), stack(5), part(4), stack(6), part(5), stack(7)]
    jobs += [("scores", H), part(6), ("scores", H + 1), part(7), ("out_turn", 0)]
    return jobs


ORDER = product_jobs()
JOBS = [job for job in ORDER if job[0] != "out" or job[1] == 0]
SLOTS = -(-len(JOBS) // BANKS) * BANKS

READ_BY = {
    "gates": "gates_taken", "qm": "qm_split", "vh": "vh_copied", "scores": "scores_masked",
    "turn": "et_copied", "layer1": "layer1_copied", "gate_up": "silu_made", "up": "hidden_made",
    "down": "down_added", "layer2": "z_copied", "weigh2": "weigh2_scaled", "stack": "stack_split",
    "x_turn": "xt_split", "out": "y_copied", "out_turn": "y_normed",
}

AHEAD = {"gates": 1, "gates_taken": 1, "qm": 2, "qm_copied": 2, "qm_split": 2, "scores": 2, "out_turn": 1}
VECTOR_LINKS = 30

PER_SEQ = {
    "gates": 1, "qm": PAIRS, "vh": PAIRS, "scores": H, "turn": H, "layer1": H, "gate_up": E, "up": E,
    "down": E, "layer2": 4, "weigh2": 4, "stack": PAIRS, "x_turn": 1, "out": PAIRS, "out_turn": 1,
    "vh_copied": PAIRS,
    "gates_taken": 1, "ez_done": 1, "qm_copied": PAIRS, "exp_done": 2 * H, "et_copied": H, "layer1_copied": H,
    "tanh_done": E, "gelu1_done": 2, "z_copied": 4, "gelu2_done": 2, "stack_copied": PAIRS,
    "xt_copied": 1, "y_copied": 1,
    "scores_masked": H, "negmax_done": PAIRS, "diag_set": PAIRS, "silu_made": E,
    "hidden_made": E, "down_added": E, "norms_done": 2, "layer1_sum": 2,
    "weigh2_scaled": 4, "y_normed": 1, "var_eps": 3, "xa_done": 1, "chain": VECTOR_LINKS, "qm_split": PAIRS,
    "stack_split": PAIRS, "xt_split": 1, "x_taken": 1,
    "v_biased": 2, "values_out": 2, "f1_biased": 2, "layer2_sum": 2, "rstd_done": 3, "result_done": 1,
    "pool_chain": 3,
    "result_left": 1,
}


def build(nc, x, gamma_in, Wq, Wk, Wv, gnn_w, gnn_b, lin_w, lin_b, Wo, gamma_out,
          Wg, Ws1, Ws3, Ws2, We1, We3, We2, out):
    B = x.shape[0]
    DM = x.shape[2]
    F = C * P
    FE = E * F
    assert x.shape[1] == T * P and DM == P

    with ExitStack() as ctx:
        def sb(name, shape, dt=F32):
            return ctx.enter_context(nc.sbuf_tensor(name, shape, dt))

        def halves(name, shape):
            return sb(name + "_hi", shape, F32R), sb(name + "_lo", shape, F32R)

        def plain(ap):
            return ap.bitcast(F32)

        sem = {n: ctx.enter_context(nc.semaphore(n)) for n in PER_SEQ}
        once = {n: ctx.enter_context(nc.semaphore(n)) for n in (
            "ld_x0", "x_loaded", "ld_q", "ld_v", "ld_g", "ld_o", "ld_e", "ld_raw", "pool_setup", "setup_product",
            "act_setup", "dve_setup", "vh_w_split", "ffn_w_split", "o_w_split", "pool_link",
            "counters_set", "stored", "first_var_eps", "first_rstd", "first_xa", "dve_chain")}

        def need(eng, b, name, count):
            assert 0 <= count <= PER_SEQ[name] + AHEAD.get(name, 0), (name, count)
            if b is None:
                eng.wait_ge(sem[name], count - PER_SEQ[name] + 1)
            else:
                eng.wait_ge(sem[name], b * PER_SEQ[name] + count + 1)

        psum = ctx.enter_context(nc.psum_tensor("psum", [P, BANKS, 512], F32))
        slot = {job: n for n, job in enumerate(JOBS)}

        def bank(kind, i):
            if (kind, i) not in slot:
                i += PER_SEQ[kind]
            return psum[:, slot[kind, i] % BANKS, :]

        ident = sb("ident", [P, P])
        mask1 = sb("mask1", [P, 2 * P])
        mask0 = mask1[:, P:2 * P]
        rank = sb("rank", [P, 8])
        minus_half = sb("minus_half", [P, T])
        gamma_col = sb("gamma_col", [P, 1])
        gamma_out_row = sb("gamma_out_row", [P, P])
        b1_row = sb("b1_row", [P, DH])
        b2_row = sb("b2_row", [P, DH])
        lin_b_col = sb("lin_b_col", [DH, 1])
        w2_2 = sb("w2_2", [P, P])
        m_w = halves("m_w", [P, H, P])
        vh_w = halves("vh_w", [P, H, 2 * DH])
        o_w = halves("o_w", [P, H, P])
        out_bias = sb("out_bias", [P, 1])
        wg = halves("wg", [P, 8])
        w_gate = halves("w_gate", [P, E, F])
        w_up = halves("w_up", [P, E, F])
        w_down = sb("w_down", [P, E, C, P])

        x_in = sb("x_in", [P, T, P])
        xn = sb("xn", [P, T, P])
        xa_t0 = sb("xa_t0", [P, P])
        xa_t = halves("xa_t", [P, T * P])
        xn_t = halves("xn_t", [P, T * P])
        stats = sb("stats", [P, T, 6])
        mv = sb("mv", [P, T, 2])
        var_eps = sb("var_eps", [P, T])
        rstd = sb("rstd", [P, T])
        qm0 = sb("qm0", [P, 2, 2, P])
        qm1 = halves("qm1", [P, 2, 2, P])
        vh = sb("vh", [P, T, H, VHW])
        work = sb("work", [P, PAIRS * T * P])
        ex = work[:, 0:4 * 3 * P].rearrange("p (h k j) -> p h k j", h=4, k=3)
        mx = sb("mx", [P, H, T])
        negmax = sb("negmax", [P, H, T])
        D = sb("D", [P, H, T])
        et = sb("et", [P, H, 3 * P])
        spare = et[:].rearrange("p h n -> p (h n)")
        hd = H * DH
        wt = spare[:, 0:3 * hd].rearrange("p (k q d) -> p k q d", k=3, q=PAIRS)
        wq, wk, wv = (spare[:, n * hd:(n + 1) * hd] for n in (3, 4, 5))
        l1 = sb("l1", [P, H, T, VHW])
        rD = sb("rD", [P, H, T])
        rG = sb("rG", [P, H, T])
        kV = sb("kV", [P, H, T])
        h1 = sb("h1", [P, T, H, DH])
        h2 = h1
        f1 = sb("f1", [P, T, H, DH])
        zt = work[:, 0:PAIRS * T * P].rearrange("p (q n) -> p q n", q=PAIRS)
        of = l1
        vo = vh[:, :, :, DH:2 * DH]
        of_t = halves("of_t", [P, STACKS, 2 * T * P])
        ys = sb("ys", [P, 2, T * P])
        y_t = ys[:, 0, :]
        xa = y_t.rearrange("p (t d) -> p t d", t=T)
        yn = ys[:, 1, :].rearrange("p (t d) -> p t d", t=T)
        hid = sb("hid", [P, 2, C * T * P])
        s_raw = hid[:, 0, :].rearrange("p (k f) -> p k f", k=2)
        wg_raw = hid[:, 1, 0:8]
        g_raw = h1[:].rearrange("p t h d -> p (t h d)").rearrange("p (e f) -> p e f", f=F)
        u_raw = f1[:].rearrange("p t h d -> p (t h d)").rearrange("p (e f) -> p e f", f=F)
        wo_raw = l1[:].rearrange("p h t d -> p (h t d)")[0:DH, 0:H * P].rearrange("p (h n) -> p h n", h=H)
        ones, w1_2 = work[:, 0:P], work[:, P:2 * P]
        lin_sb, lin_t = (work[0:DH, n * P:n * P + DH] for n in (2, 3))
        ffn = sb("ffn", [P, T, P])
        z_exp = sb("z_exp", [P, T, 8])
        ez = sb("ez", [P, T, 8])
        gates = sb("gates_sb", [P, T, 8])
        gw = sb("gw", [P, 8, T, 8])
        gv = sb("gv", [P, 6, T])
        w_exp = sb("w_exp", [P, T, 8])
        carrier = sb("carrier", [P, 48])

        x_dram = x.rearrange("b (t p) d -> b p t d", p=P)
        out_dram = out.rearrange("b (t p) d -> b p t d", p=P)

        block = ctx.enter_context(nc.Block())

        def bc(ap, n):
            return ap.unsqueeze(len(ap.shape)).to_broadcast(list(ap.shape) + [n])

        def heads_t(ap):
            return ap.rearrange("p h t -> p t h")

        LOADS = dict(ld_x0=1, ld_q=2, ld_v=7, ld_g=3, ld_o=3, ld_e=3, ld_raw=4)

        def loaded(eng, name):
            eng.wait_ge(once[name], 16 * LOADS[name])

        @block.sync
        def _(sp):
            sp.dma_start(x_in[:], x_dram[0]).then_inc(once["ld_x0"], 16)
            sp.dma_start(wq, Wq).then_inc(once["ld_q"], 16)
            sp.dma_start(wv, Wv).then_inc(once["ld_v"], 16)
            sp.wait_ge(once["pool_setup"], 2)
            for n in range(2):
                for k, w in ((0, w1_2), (1, w2_2)):
                    sp.dma_start(w[n * DH:(n + 1) * DH, n * DH:(n + 1) * DH], gnn_w[k]).then_inc(once["ld_v"], 16)
            sp.dma_start(b1_row[:], gnn_b[0].partition_broadcast(P)).then_inc(once["ld_v"], 16)
            sp.dma_start(s_raw[:, 0, :], Ws1).then_inc(once["ld_raw"], 16)
            sp.dma_start(s_raw[:, 1, :], Ws3).then_inc(once["ld_raw"], 16)
            sp.dma_start(u_raw, We3.rearrange("e d f -> d e f")).then_inc(once["ld_raw"], 16)
            sp.dma_start(w_down[:, 0], Ws2.rearrange("(c p) d -> p c d", p=P)).then_inc(once["ld_e"], 16)
            sp.dma_start(w_down[:, 1:5], We2[0:4].rearrange("e (c p) d -> p e c d", p=P)).then_inc(once["ld_e"], 16)
            sp.dma_start(w_down[:, 5:9], We2[4:8].rearrange("e (c p) d -> p e c d", p=P)).then_inc(once["ld_e"], 16)
            for n in sem:
                sp.sem_inc(sem[n], 1)
            sp.sem_inc(once["counters_set"], 1)
            with sp.Fori(0, B) as b:
                need(sp, b, "result_done", 1)
                sp.dma_start(out_dram[(b + B - 1) % B], yn).then_inc(once["stored"], 16)
                sp.wait_ge(once["stored"], b * 16 + 16)
                sp.sem_inc(sem["result_left"], 1)
                need(sp, b, "x_taken", 1)
                sp.dma_start(x_in[:], x_dram[(b + 1) % B]).then_inc(once["x_loaded"], 16)
            need(sp, B, "result_done", 1)
            sp.dma_start(out_dram[B - 1], yn).then_inc(once["stored"], 16)
            sp.wait_ge(once["stored"], 16 * (B + 1))
            sp.wait_ge(once["x_loaded"], 16 * B)

        SETUP = (["x_turn"] + ["w_turn"] * 6 + ["m"] * 4 + ["vw1"] * 2 + ["lin_turn"] + ["lin_wo"] * 4 + ["bias"])
        first = {k: SETUP.index(k) for k in SETUP}

        def by_act(n):
            return SETUP[n] != "w_turn" or (n - first["w_turn"]) % 2 == 0

        def by_dve(n):
            return not by_act(n) or SETUP[n] not in ("w_turn", "lin_turn", "bias")

        def emptied(eng, n):
            eng.wait_ge(once["act_setup"], sum(map(by_act, range(n + 1))))
            if any(map(by_dve, range(n + 1))):
                eng.wait_ge(once["dve_setup"], sum(map(by_dve, range(n + 1))))

        def setup_targets(n):
            src = psum[:, n % BANKS, :]
            kind, k = SETUP[n], n - first[SETUP[n]]
            by4 = src.rearrange("p (q d) -> p q d", q=4)
            if kind == "w_turn":
                return [(wt.rearrange("p k q d -> p (k q) d")[:, 4 * k:4 * k + 4, :], None, by4, 1.0)]
            if kind == "m":
                at = slice(8 * (k // 2) + k % 2, 8 * (k // 2) + 8, 2)
                return [(m_w[0][:, at, :], m_w[1][:, at, :], by4, DH ** -0.5)]
            if kind == "vw1":
                hi, lo = (w[:, 8 * k:8 * k + 8, DH:2 * DH] for w in vh_w)
                return [(hi, lo, src.rearrange("p (q d) -> p q d", q=8), 1.0)]
            if kind == "lin_turn":
                return [(lin_t, None, src[0:DH, 0:DH], 1.0)]
            if kind == "lin_wo":
                hi, lo = (w[DH:P, 4 * k:4 * k + 4, :] for w in o_w)
                return [(hi, lo, by4[DH:P], 1.0)]
            return [(out_bias[:], None, src[:, 0:1], 1.0)]

        def turned_by_act(src):
            nc.scalar.activation(xa_t[0][:], src[:, 0:T * P], ACT.Copy, scale=gamma_col[:, 0:1])
            return nc.scalar.copy(xn_t[0][:], src[:, T * P:2 * T * P])

        def turned_by_dve(src):
            nc.vector.scalar_tensor_tensor(out=xa_t[1][:], in0=src[:, 0:T * P], scalar=gamma_col[:, 0:1],
                                           in1=plain(xa_t[0][:]), op0=ALU.mult, op1=ALU.subtract)
            nc.vector.tensor_tensor(xn_t[1][:], src[:, T * P:2 * T * P], plain(xn_t[0][:]), ALU.subtract)
            return nc.vector.tensor_scalar(xa_t0[:], src[:, 0:P], gamma_col[:, 0:1], None, ALU.mult)

        @block.gpsimd
        def _(pool):
            pool.memset(w1_2, 0.0).then_inc(once["pool_setup"], 1)
            pool.memset(w2_2[:], 0.0).then_inc(once["pool_setup"], 1)
            pool.memset(minus_half[:], -0.5)
            pool.memset(ffn[:], 0.0)
            pool.memset(mask1[:], 0.0)
            pool.memset(vh[:, :, :, 2 * DH:VHW], 1.0)
            pool.memset(ones, 1.0).then_inc(once["pool_setup"], 1)
            pool.iota(rank[:], pattern=[[-1, 8]], base=8, channel_multiplier=0,
                      allow_small_or_imprecise_dtypes=True)
            pool.wait_ge(once["pool_setup"], 3)
            pool.affine_select(out=ident[:], in_=ones, compare_op=ALU.is_equal, fill=0.0, base=0,
                               pattern=[[-1, P]], channel_multiplier=1)
            pool.affine_select(out=mask1[:, P:2 * P], in_=mask1[:, P:2 * P], compare_op=ALU.is_ge,
                               fill=MASKED, base=0, pattern=[[-1, P]],
                               channel_multiplier=1).then_inc(once["pool_setup"], 1)
            for n in range(2):
                pool.wait_ge(once["first_var_eps"], n + 1)
                pool.tensor_tensor(rstd[:], var_eps[:], minus_half[:], ALU.pow).then_inc(once["first_rstd"], 1)
            split_count = [0]

            def split(pair, raw, signal):
                hi, lo = pair
                split_count[0] += 1
                pool.tensor_copy(hi, raw).then_inc(once["pool_link"], 1)
                pool.wait_ge(once["pool_link"], split_count[0])
                ins = pool.tensor_tensor(lo, raw, plain(hi), ALU.subtract)
                if signal:
                    ins.then_inc(once[signal], 1)

            loaded(pool, "ld_v")
            split([w[:] for w in wg], wg_raw, None)
            split([w[:, :, 0:DH] for w in vh_w], wv.rearrange("p (h d) -> p h d", h=H), "vh_w_split")
            loaded(pool, "ld_o")
            split([w[0:DH] for w in o_w], wo_raw, "o_w_split")
            loaded(pool, "ld_raw")
            split([w[:, 0, :] for w in w_gate], s_raw[:, 0, :], None)
            split([w[:, 0, :] for w in w_up], s_raw[:, 1, :], None)
            split([w[:, 1:E, :] for w in w_gate], g_raw, None)
            split([w[:, 1:E, :] for w in w_up], u_raw, "ffn_w_split")
            loaded(pool, "ld_g")

            def rstd_of(b, n):
                need(pool, b, "var_eps", n + 1)
                pool.tensor_tensor(rstd[:], var_eps[:], minus_half[:], ALU.pow).then_inc(sem["rstd_done"], 1)

            pool.wait_ge(once["counters_set"], 1)
            def finish(b):
                rstd_of(b, 0)
                need(pool, b, "down_added", 0)
                need(pool, b, "y_normed", 1)
                pool.tensor_tensor(yn, yn, gamma_out_row[:].unsqueeze(1).to_broadcast([P, T, P]),
                                   ALU.mult).then_inc(sem["pool_chain"], 1)
                need(pool, b, "pool_chain", 1)
                pool.tensor_tensor(yn, yn, ffn[:], ALU.add).then_inc(sem["result_done"], 1)

            with pool.Fori(0, B) as b:
                finish(b)
                def bias_v(hf):
                    hs = slice(hf * PAIRS, (hf + 1) * PAIRS)
                    need(pool, b, "vh_copied", 4 * hf + 4)
                    if hf == 0:
                        need(pool, b, "gelu2_done", 0)
                    pool.tensor_tensor(h1[:, :, hs, :], vh[:, :, hs, 0:DH],
                                       b1_row[:].unsqueeze(1).unsqueeze(1).to_broadcast([P, T, PAIRS, DH]),
                                       ALU.add).then_inc(sem["v_biased"], 1)

                bias_v(0)
                rstd_of(b, 1)
                rstd_of(b, 2)
                bias_v(1)
                for hf in range(2):
                    hs = slice(hf * PAIRS, (hf + 1) * PAIRS)
                    need(pool, b, "norms_done", hf + 1)
                    pool.tensor_tensor(vo[:, :, hs], vh[:, :, hs, 0:DH], bc(heads_t(kV[:, hs]), DH), ALU.mult)
                    values = of[:, hs, :, 0:DH].rearrange("p h t d -> p t h d")
                    pool.tensor_tensor(values, values,
                                       bc(heads_t(rD[:, hs]), DH), ALU.mult).then_inc(sem["pool_chain"], 1)
                    need(pool, b, "pool_chain", hf + 2)
                    pool.tensor_tensor(values, values, vo[:, :, hs], ALU.add).then_inc(sem["values_out"], 1)
                for hf in range(2):
                    hs = slice(hf * PAIRS, (hf + 1) * PAIRS)
                    need(pool, b, "layer2", 2 * hf + 2)
                    pool.tensor_tensor(f1[:, :, hs, :], f1[:, :, hs, :],
                                       b2_row[:].unsqueeze(1).unsqueeze(1).to_broadcast([P, T, PAIRS, DH]),
                                       ALU.add).then_inc(sem["f1_biased"], 1)
                for hf in range(2):
                    hs = slice(hf * PAIRS, (hf + 1) * PAIRS)
                    need(pool, b, "weigh2_scaled", 2 * hf + 2)
                    need(pool, b, "f1_biased", hf + 1)
                    pool.tensor_tensor(h2[:, :, hs, :], h2[:, :, hs, :], f1[:, :, hs, :],
                                       ALU.add).then_inc(sem["layer2_sum"], 1)
            finish(B)

        @block.scalar
        def _(act):
            act.dma_start(gamma_col[:], gamma_in.rearrange("(p o) -> p o", o=1)).then_inc(once["ld_g"], 16)
            act.dma_start(wk, Wk).then_inc(once["ld_q"], 16)
            act.dma_start(wo_raw, Wo.rearrange("(h p) n -> p h n", p=DH)).then_inc(once["ld_o"], 16)
            act.dma_start(lin_sb, lin_w).then_inc(once["ld_o"], 16)
            act.dma_start(lin_b_col[:], lin_b.rearrange("(p o) -> p o", o=1)).then_inc(once["ld_o"], 16)
            act.dma_start(b2_row[:], gnn_b[1].partition_broadcast(P)).then_inc(once["ld_g"], 16)
            act.dma_start(gamma_out_row[:], gamma_out.partition_broadcast(P)).then_inc(once["ld_g"], 16)
            act.dma_start(wg_raw, Wg).then_inc(once["ld_v"], 16)
            act.dma_start(g_raw, We1.rearrange("e d f -> d e f")).then_inc(once["ld_raw"], 16)
            loaded(act, "ld_g")
            for n in range(len(SETUP)):
                if by_act(n):
                    act.wait_ge(once["setup_product"], n + 1)
                    if SETUP[n] == "x_turn":
                        ins = turned_by_act(psum[:, n % BANKS, :])
                    else:
                        for whole, _, src, scale in setup_targets(n):
                            ins = nc.scalar.activation(whole, src, ACT.Copy, scale=scale)
                    ins.then_inc(once["act_setup"], 1)

            def read(b, kind, n):
                need(act, b, kind, n + 1)
                return bank(kind, 0 if kind == "out" else n)

            def copy_qm(b, p):
                need(act, b, "qm", p + 1)
                src = bank("qm", p).rearrange("p (a n) -> p a n", a=2)
                if b is not None:
                    need(act, b, "scores", 2 * p - 2)
                nc.scalar.copy(qm0[:, p % 2], src[:, :, 0:P])
                nc.scalar.copy(qm1[0][:, p % 2], src[:, :, P:2 * P]).then_inc(sem["qm_copied"], 1)

            def take_gates(src):
                nc.scalar.copy(z_exp[:], src[:, 0:T * 8].rearrange("p (t e) -> p t e", t=T)
                               ).then_inc(sem["gates_taken"], 1)

            def exp_gates(b):
                need(act, b, "gates_taken", 1)
                nc.scalar.activation(ez[:], z_exp[:], ACT.Exp, scale=-1.0).then_inc(sem["ez_done"], 1)

            def exps(b, h):
                need(act, b, "negmax_done", h // 2 + 1)
                for t in range(T):
                    blocks = slice(0, 1) if t == 0 else slice(1, 3)
                    e = ex[:, h % 4, blocks, :].rearrange("p k j -> p (k j)")
                    nc.scalar.activation(e, e, ACT.Exp, bias=negmax[:, h, t:t + 1], scale=1.0,
                                         accum_out=D[:, h, t:t + 1]).then_inc(sem["exp_done"], 1)

            def copy_et(b, h):
                src = read(b, "turn", h)
                nc.scalar.copy(et[:, h, :], src[:, 0:3 * P]).then_inc(sem["et_copied"], 1)

            def copy_vh(b, n):
                q, t = n // 2, n % 2
                src = read(b, "vh", n)
                nc.scalar.copy(vh[:, t, 4 * q:4 * q + 4, 0:2 * DH], src.rearrange("p (h d) -> p h d", h=4)
                               ).then_inc(sem["vh_copied"], 1)

            def copy_l1(b, h):
                src = read(b, "layer1", h)
                if h == 0:
                    act.wait_ge(once["o_w_split"], 1)
                nc.scalar.copy(l1[:, h, :, :], src[:, 0:T * VHW].rearrange("p (t d) -> p t d", t=T)
                               ).then_inc(sem["layer1_copied"], 1)

            def tanh(b, e):
                src = read(b, "gate_up", e)
                need(act, b, "down", max(e - 1, 0))
                nc.scalar.activation(hid[:, e % 2, :], src, ACT.Tanh, scale=0.5).then_inc(sem["tanh_done"], 1)

            def gelu1(b, hf):
                hs = slice(hf * PAIRS, (hf + 1) * PAIRS)
                need(act, b, "layer1_sum", hf + 1)
                nc.scalar.activation(f1[:, :, hs, :], h1[:, :, hs, :], ACT.Gelu).then_inc(sem["gelu1_done"], 1)

            def gelu2(b, hf):
                hs = slice(hf * PAIRS, (hf + 1) * PAIRS)
                need(act, b, "layer2_sum", hf + 1)
                nc.scalar.activation(of[:, hs, :, DH:2 * DH].rearrange("p h t d -> p t h d"), h2[:, :, hs, :],
                                     ACT.Gelu).then_inc(sem["gelu2_done"], 1)

            def copy_z(b, g):
                src = read(b, "layer2", g)
                nc.scalar.copy(zt[:, 2 * g:2 * g + 2, :].rearrange("p q n -> p (q n)"), src
                               ).then_inc(sem["z_copied"], 1)

            def copy_stack(b, p):
                src = read(b, "stack", p)
                if p >= STACKS:
                    need(act, b, "out", p - STACKS + 1)
                nc.scalar.copy(of_t[0][:, p % STACKS, :], src).then_inc(sem["stack_copied"], 1)

            act.wait_ge(once["counters_set"], 1)
            need(act, None, "gates", 2)
            take_gates(bank("gates", 1))
            copy_qm(None, PAIRS)
            copy_qm(None, PAIRS + 1)
            with act.Fori(0, B) as b:
                need(act, b, "norms_done", 0)
                need(act, b, "values_out", 0)
                exps(b, 0)
                exps(b, 1)
                exp_gates(b)
                for s in range(PAIRS):
                    if s >= 1:
                        copy_et(b, 2 * s - 2)
                        copy_et(b, 2 * s - 1)
                    copy_vh(b, s)
                    if s + 2 < PAIRS:
                        copy_qm(b, s + 2)
                    if s + 1 < PAIRS:
                        exps(b, 2 * s + 2)
                    if s >= 2:
                        tanh(b, s - 2)
                    if s + 1 < PAIRS:
                        exps(b, 2 * s + 3)
                    if s >= 1:
                        copy_l1(b, 2 * s - 2)
                        copy_l1(b, 2 * s - 1)
                copy_et(b, H - 2)
                copy_et(b, H - 1)
                tanh(b, 6)
                gelu1(b, 0)
                copy_l1(b, H - 2)
                copy_l1(b, H - 1)
                copy_z(b, 0)
                copy_z(b, 1)
                tanh(b, 7)
                gelu1(b, 1)
                copy_z(b, 2)
                copy_z(b, 3)
                tanh(b, 8)
                turned_by_act(read(b, "x_turn", 0)).then_inc(sem["xt_copied"], 1)
                gelu2(b, 0)
                take_gates(read(b, "gates", 1))
                copy_qm(b, PAIRS)
                copy_stack(b, 0)
                copy_qm(b, PAIRS + 1)
                copy_stack(b, 1)
                gelu2(b, 1)
                for p in range(2, 8):
                    copy_stack(b, p)
                src = read(b, "out", PAIRS - 1)
                nc.scalar.activation(y_t, src[:, 0:T * P], ACT.Identity, bias=out_bias[:, 0:1]
                                     ).then_inc(sem["y_copied"], 1)

        @block.vector
        def _(dve):
            V = nc.vector

            carried = [0]

            def carry_wait():
                carried[0] += 1
                return V.memset(carrier[:, carried[0] - 1:carried[0]], 0.0)

            def mean_var(n, src, link):
                for t in range(T):
                    ins = V.bn_stats(stats[:, t, :], src(t))
                link(ins)
                carry_wait()
                for t in range(T):
                    ins = V.bn_aggr(mv[:, t, :], stats[:, t, :])
                link(ins)
                return V.tensor_scalar(var_eps[:], mv[:, :, 1], EPS, None, ALU.add)

            def normed(dst, src):
                for t in range(T):
                    ins = V.tensor_scalar(dst(t), src(t), mv[:, t, 0:1], rstd[:, t:t + 1], ALU.subtract, ALU.mult)
                return ins

            links = [0]

            def link_once(ins):
                links[0] += 1
                ins.then_inc(once["dve_chain"], 1)
                dve.wait_ge(once["dve_chain"], links[0])

            loaded(dve, "ld_x0")
            mean_var(0, lambda t: x_in[:, t, :], link_once).then_inc(once["first_var_eps"], 1)
            dve.wait_ge(once["first_rstd"], 1)
            link_once(normed(lambda t: xn[:, t, :], lambda t: x_in[:, t, :]))
            mean_var(1, lambda t: xn[:, t, :], link_once).then_inc(once["first_var_eps"], 1)
            dve.wait_ge(once["first_rstd"], 2)
            normed(lambda t: xa[:, t, :], lambda t: xn[:, t, :]).then_inc(once["first_xa"], 1)
            loaded(dve, "ld_g")
            loaded(dve, "ld_v")
            dve.wait_ge(once["pool_setup"], 4)
            for n in range(len(SETUP)):
                if by_dve(n):
                    dve.wait_ge(once["setup_product"], n + 1)
                    if by_act(n):
                        emptied_by_act = sum(map(by_act, range(n + 1)))
                        dve.wait_ge(once["act_setup"], emptied_by_act)
                    if SETUP[n] == "x_turn":
                        ins = turned_by_dve(psum[:, n % BANKS, :])
                    else:
                        for hi, lo, src, scale in setup_targets(n):
                            if lo is None:
                                ins = V.tensor_copy(hi, src)
                            else:
                                ins = V.scalar_tensor_tensor(out=lo, in0=src, scalar=scale, in1=plain(hi),
                                                             op0=ALU.mult, op1=ALU.subtract)
                    ins.then_inc(once["dve_setup"], 1)

            def read(b, kind, n):
                need(dve, b, kind, n + 1)
                return bank(kind, n)

            def mask_scores(b, p):
                for h in (2 * p, 2 * p + 1):
                    src = read(b, "scores", h)
                    need(dve, b, "turn", max(h - 3, 0))
                    carry_wait()
                    V.tensor_tensor_reduce(ex[:, h % 4, 0, :], src[:, 0:P], mask0, 1.0, MASKED,
                                           ALU.add, ALU.max, mx[:, h, 0:1])
                    V.tensor_tensor_reduce(ex[:, h % 4, 1:3, :].rearrange("p k j -> p (k j)"), src[:, P:3 * P], mask1[:], 1.0, MASKED,
                                           ALU.add, ALU.max, mx[:, h, 1:2]).then_inc(sem["scores_masked"], 1)
                need(dve, b, "scores_masked", 2 * p + 2)
                V.tensor_scalar(negmax[:, 2 * p:2 * p + 2, :], mx[:, 2 * p:2 * p + 2, :], -1.0, None,
                                ALU.mult).then_inc(sem["negmax_done"], 1)

            def split_qm(b, p):
                need(dve, b, "qm_copied", p + 1)
                src = bank("qm", p).rearrange("p (a n) -> p a n", a=2)
                V.tensor_tensor(qm1[1][:, p % 2], src[:, :, P:2 * P], plain(qm1[0][:, p % 2]),
                                ALU.subtract).then_inc(sem["qm_split"], 1)

            def split_stack(b, p):
                need(dve, b, "stack_copied", p + 1)
                V.tensor_tensor(of_t[1][:, p % STACKS, :], bank("stack", p), plain(of_t[0][:, p % STACKS, :]),
                                ALU.subtract).then_inc(sem["stack_split"], 1)

            def set_diagonal(b, p):
                need(dve, b, "exp_done", 4 * p + 4)
                carry_wait()
                r = 2 * (p % 2)
                V.copy_predicated(ex[:, r:r + 2, 0:3:2, :],
                                  ident[:].bitcast(U32).unsqueeze(1).unsqueeze(1).to_broadcast([P, 2, 2, P]),
                                  bc(D[:, 2 * p:2 * p + 2, :], P)).then_inc(sem["diag_set"], 1)

            def norms(b, hf, link):
                hs = slice(hf * PAIRS, (hf + 1) * PAIRS)
                need(dve, b, "layer1_copied", PAIRS * (hf + 1))
                V.reciprocal(rG[:, hs], l1[:, hs, :, 2 * DH])
                link(V.reciprocal(rD[:, hs], D[:, hs]))
                link(V.tensor_tensor(kV[:, hs], l1[:, hs, :, 2 * DH], rD[:, hs], ALU.mult))
                V.tensor_scalar(kV[:, hs], kV[:, hs], -1.0, 1.0, ALU.mult, ALU.add).then_inc(sem["norms_done"], 1)

            def scale_layer1(b, hf, link):
                hs = slice(hf * PAIRS, (hf + 1) * PAIRS)
                weighed = l1[:, hs, :, DH:2 * DH].rearrange("p h t d -> p t h d")
                link(V.tensor_tensor(weighed, weighed, bc(heads_t(rG[:, hs]), DH), ALU.mult))
                need(dve, b, "v_biased", hf + 1)
                V.tensor_tensor(h1[:, :, hs, :], weighed, h1[:, :, hs, :], ALU.add).then_inc(sem["layer1_sum"], 1)

            def choose(b, part, link):
                need(dve, b, "ez_done", 1)
                g, m, s1, o1, g2, s2, o2 = (gw[:, i] for i in range(7))
                v1, v2, p1, p2, den, rden = (gv[:, i] for i in range(6))
                ranks = rank[:].unsqueeze(1).to_broadcast([P, T, 8])
                if part == 0:
                    link(V.tensor_scalar(g, ez[:], 1.0, None, ALU.add))
                    link(V.reciprocal(gates[:], g))
                    link(V.tensor_reduce(v1, gates[:], AX_X, ALU.max))
                    link(V.tensor_tensor(m, gates[:], bc(v1, 8), ALU.is_equal))
                    link(V.tensor_tensor(s1, m, ranks, ALU.mult))
                    link(V.tensor_reduce(p1, s1, AX_X, ALU.max))
                    link(V.tensor_tensor(o1, s1, bc(p1, 8), ALU.is_equal))
                elif part == 1:
                    link(V.scalar_tensor_tensor(out=g2, in0=o1, scalar=-4.0, in1=gates[:], op0=ALU.mult, op1=ALU.add))
                    link(V.tensor_reduce(v2, g2, AX_X, ALU.max))
                    link(V.tensor_tensor(m, g2, bc(v2, 8), ALU.is_equal))
                    link(V.tensor_tensor(s2, m, ranks, ALU.mult))
                    link(V.tensor_reduce(p2, s2, AX_X, ALU.max))
                    link(V.tensor_tensor(o2, s2, bc(p2, 8), ALU.is_equal))
                else:
                    V.tensor_tensor(den, v1, v2, ALU.add)
                    link(V.tensor_tensor(m, o1, o2, ALU.add))
                    V.reciprocal(rden, den)
                    link(V.tensor_tensor(s2, m, gates[:], ALU.mult))
                    link(V.tensor_tensor(s1, s2, bc(rden, 8), ALU.mult))
                    link(V.tensor_scalar(w_exp[:], s1, 0.5 / 3.0, None, ALU.mult))

            def hidden(b, e):
                g = bank("gate_up", e)
                need(dve, b, "tanh_done", e + 1)
                V.scalar_tensor_tensor(out=hid[:, e % 2, :], in0=hid[:, e % 2, :], scalar=1.0, in1=g,
                                       op0=ALU.add, op1=ALU.mult).then_inc(sem["silu_made"], 1)
                u = read(b, "up", e)
                need(dve, b, "silu_made", e + 1)
                V.tensor_tensor(hid[:, e % 2, :], hid[:, e % 2, :], u, ALU.mult).then_inc(sem["hidden_made"], 1)

            def add_down(b, e):
                src = read(b, "down", e)
                if e == 0:
                    need(dve, b, "result_done", 1)
                    V.scalar_tensor_tensor(out=ffn[:], in0=src[:, 0:T * P].rearrange("p (t d) -> p t d", t=T),
                                           scalar=0.5 / 3.0, in1=x_in[:], op0=ALU.mult,
                                           op1=ALU.add).then_inc(sem["down_added"], 1)
                    need(dve, b, "down_added", 1)
                    carry_wait().then_inc(sem["x_taken"], 1)
                    return
                need(dve, b, "down_added", e)
                for t in range(T):
                    ins = V.scalar_tensor_tensor(out=ffn[:, t, :], in0=src[:, t * P:(t + 1) * P],
                                                 scalar=w_exp[:, t, e - 1:e], in1=ffn[:, t, :],
                                                 op0=ALU.mult, op1=ALU.add)
                ins.then_inc(sem["down_added"], 1)

            def scale_weigh2(b, n):
                q, t = n // 2, n % 2
                hs = slice(q * PAIRS, (q + 1) * PAIRS)
                src = read(b, "weigh2", n)
                V.tensor_tensor(h2[:, t, hs, :], src.rearrange("p (h d) -> p h d", h=PAIRS),
                                bc(rG[:, hs, t], DH), ALU.mult).then_inc(sem["weigh2_scaled"], 1)

            dve.wait_ge(once["counters_set"], 1)
            split_qm(None, PAIRS)
            split_qm(None, PAIRS + 1)
            count = [0]

            def linker(b):
                def link(ins):
                    count[0] += 1
                    ins.then_inc(sem["chain"], 1)
                    need(dve, b, "chain", count[0])
                return link

            y = bank("out_turn", 0)

            def finish_stats(b, link):
                need(dve, b, "out_turn", 1)
                mean_var(2, lambda t: y[:, t * P:(t + 1) * P], link).then_inc(sem["var_eps"], 1)

            def finish_norm(b):
                need(dve, b, "result_left", 0)
                need(dve, b, "rstd_done", 1)
                normed(lambda t: yn[:, t, :], lambda t: y[:, t * P:(t + 1) * P]).then_inc(sem["y_normed"], 1)

            with dve.Fori(0, B) as b:
                link = linker(b)
                mask_scores(b, 0)
                finish_stats(b, link)
                for s in range(PAIRS):
                    if s == 1:
                        finish_norm(b)
                    if s >= 1:
                        set_diagonal(b, s)
                    if s >= 4:
                        add_down(b, s - 4)
                    if 1 <= s <= 3:
                        choose(b, s - 1, link)
                    if s == 5:
                        dve.wait_ge(once["x_loaded"], b * 16 + 16)
                        mean_var(0, lambda t: x_in[:, t, :], link).then_inc(sem["var_eps"], 1)
                    if s == 6:
                        need(dve, b, "rstd_done", 2)
                        link(normed(lambda t: xn[:, t, :], lambda t: x_in[:, t, :]))
                        mean_var(1, lambda t: xn[:, t, :], link).then_inc(sem["var_eps"], 1)
                    if s + 1 < PAIRS:
                        mask_scores(b, s + 1)
                    if s == 0:
                        set_diagonal(b, s)
                    if s == 6:
                        norms(b, 0, link)
                    if s + 2 < PAIRS:
                        split_qm(b, s + 2)
                    if s >= 2:
                        hidden(b, s - 2)
                    if s == 7:
                        need(dve, b, "rstd_done", 3)
                        normed(lambda t: xa[:, t, :], lambda t: xn[:, t, :]).then_inc(sem["xa_done"], 1)
                        scale_layer1(b, 0, link)
                add_down(b, 4)
                hidden(b, 6)
                norms(b, 1, link)
                scale_layer1(b, 1, link)
                add_down(b, 5)
                hidden(b, 7)
                scale_weigh2(b, 0)
                scale_weigh2(b, 1)
                add_down(b, 6)
                hidden(b, 8)
                add_down(b, 7)
                need(dve, b, "xt_copied", 1)
                turned_by_dve(bank("x_turn", 0)).then_inc(sem["xt_split"], 1)
                scale_weigh2(b, 2)
                scale_weigh2(b, 3)
                split_qm(b, PAIRS)
                split_stack(b, 0)
                split_qm(b, PAIRS + 1)
                split_stack(b, 1)
                add_down(b, 8)
                for p in range(2, 8):
                    split_stack(b, p)
                assert count[0] == VECTOR_LINKS, count[0]
                count[0] = 0
            finish_stats(B, linker(B))
            finish_norm(B)

        @block.tensor
        def _(pe):
            def setup_bank(n):
                if n >= BANKS:
                    emptied(pe, n - BANKS)
                return psum[:, n % BANKS, :]

            pe.wait_ge(once["pool_setup"], 4)
            pe.wait_ge(once["first_xa"], 1)
            for n, kind in enumerate(SETUP):
                k = n - first[kind]
                dst = setup_bank(n)
                if kind == "x_turn":
                    for j, src in enumerate((xa, xn)):
                        for t in range(T):
                            ins = pe.transpose(dst[:, (2 * j + t) * P:(2 * j + t + 1) * P], src[:, t, :], ident[:])
                elif kind == "w_turn":
                    if k == 0:
                        loaded(pe, "ld_q")
                    if k == 4:
                        loaded(pe, "ld_v")
                    w = (wq, wk, wv)[k // 2]
                    for j in range(4):
                        p = 4 * (k % 2) + j
                        ins = pe.transpose(dst[:, j * P:(j + 1) * P], w[:, p * P:(p + 1) * P], ident[:])
                elif kind == "m":
                    if k == 0:
                        emptied(pe, first["w_turn"] + 3)
                    for j in range(4):
                        h = 8 * (k // 2) + 2 * j + k % 2
                        rows = slice(DH * (h % 2), DH * (h % 2) + DH)
                        ins = pe.matmul(dst[:, j * P:(j + 1) * P], wt[rows, 0, h // 2, :], wt[rows, 1, h // 2, :],
                                        start=True, stop=True)
                elif kind == "vw1":
                    if k == 0:
                        emptied(pe, first["w_turn"] + 5)
                    for j in range(4):
                        ins = pe.matmul(dst[:, j * P:(j + 1) * P], wt[:, 2, 4 * k + j, :], w1_2,
                                        start=True, stop=True)
                elif kind == "lin_turn":
                    loaded(pe, "ld_o")
                    ins = pe.transpose(dst[0:DH, 0:DH], lin_sb, ident[0:DH, 0:DH])
                elif kind == "lin_wo":
                    if k == 0:
                        emptied(pe, first["lin_turn"])
                    ins = pe.matmul(dst[DH:P, :], lin_t,
                                    wo_raw[:, 4 * k:4 * k + 4, :].rearrange("p h n -> p (h n)"),
                                    start=True, stop=True)
                else:
                    for h in range(H):
                        ins = pe.matmul(dst[:, 0:1], wo_raw[:, h, :], lin_b_col[:], start=h == 0, stop=h == H - 1)
                ins.then_inc(once["setup_product"], 1)
            emptied(pe, len(SETUP) - 1)
            loaded(pe, "ld_e")
            pe.wait_ge(once["vh_w_split"], 1)

            def split_product(out, a, b, a_at, b_at, start=True, stop=True):
                pe.matmul(out, a_at(a[1]), b_at(b[0]), start=start, stop=False)
                pe.matmul(out, a_at(a[0]), b_at(b[1]), start=False, stop=False)
                return pe.matmul(out, a_at(a[0]), b_at(b[0]), start=False, stop=stop)

            whole = lambda w: w[:]

            def free_bank(b, n):
                m = n - BANKS
                while m < 0 and m + SLOTS >= len(JOBS):
                    m -= BANKS
                kind, i = JOBS[m if m >= 0 else m + SLOTS]
                if kind == "out_turn":
                    need(pe, b, READ_BY[kind], 1)
                elif m >= 0:
                    need(pe, b, READ_BY[kind], i + 1)
                else:
                    need(pe, b, READ_BY[kind], max(i + 1 - PER_SEQ[READ_BY[kind]], 0))

            def product(b, kind, i):
                dst = bank(kind, 0 if kind == "out" else i)
                if kind == "gates":
                    if b is not None:
                        need(pe, b, "xt_split", 1)
                    for t in range(T):
                        ins = split_product(dst[:, t * 8:t * 8 + 8], xn_t, wg, lambda x: x[:, t * P:(t + 1) * P], whole)
                elif kind == "qm":
                    for j in range(2):
                        ins = split_product(dst[:, j * T * P:(j + 1) * T * P], m_w, xa_t,
                                            lambda w: w[:, 2 * (i % PAIRS) + j, :], whole)
                elif kind == "scores":
                    need(pe, b, "qm_split", i // 2 + 1)
                    at = lambda q: q[:, (i // 2) % 2, i % 2, :]
                    pe.matmul(dst[:, 0:P], at(qm0), xa_t0[:], start=True, stop=True)
                    ins = split_product(dst[:, P:3 * P], qm1, xa_t, at, whole)
                elif kind == "vh":
                    q, t = i // 2, i % 2
                    ins = split_product(dst, xa_t, vh_w, lambda x: x[:, t * P:(t + 1) * P],
                                        lambda w: w[:, 4 * q:4 * q + 4, :].rearrange("p h d -> p (h d)"))
                elif kind == "turn":
                    need(pe, b, "diag_set", i // 2 + 1)
                    for k in range(3):
                        ins = pe.transpose(dst[:, k * P:(k + 1) * P], ex[:, i % 4, k, :], ident[:])
                elif kind == "layer1":
                    need(pe, b, "et_copied", i + 1)
                    need(pe, b, "vh_copied", 2 * (i // 4) + 2)
                    pe.matmul(dst[:, 0:VHW], et[:, i, 0:P], vh[:, 0, i, :], start=True, stop=True)
                    pe.matmul(dst[:, VHW:2 * VHW], et[:, i, P:2 * P], vh[:, 0, i, :], start=True, stop=False)
                    ins = pe.matmul(dst[:, VHW:2 * VHW], et[:, i, 2 * P:3 * P], vh[:, 1, i, :],
                                    start=False, stop=True)
                elif kind in ("gate_up", "up"):
                    w = w_gate if kind == "gate_up" else w_up
                    if i == 0:
                        pe.wait_ge(once["ffn_w_split"], 1)
                    for c in range(C):
                        ins = split_product(dst[:, c * T * P:(c + 1) * T * P], w, xn_t,
                                            lambda w: w[:, i, c * P:(c + 1) * P], whole)
                elif kind == "down":
                    need(pe, b, "hidden_made", i + 1)
                    for t in range(T):
                        for c in range(C):
                            ins = pe.matmul(dst[:, t * P:(t + 1) * P], hid[:, i % 2, (c * T + t) * P:(c * T + t + 1) * P],
                                            w_down[:, i, c, :], start=c == 0, stop=c == C - 1)
                elif kind == "layer2":
                    need(pe, b, "gelu1_done", i // 2 + 1)
                    for j in range(2):
                        for r in range(2):
                            h = 4 * i + 2 * j + r
                            rows = slice(DH * r, DH * r + DH)
                            at = j * T * P
                            pe.matmul(dst[rows, at:at + T * P], f1[:, 0, h, :], et[:, h, 0:2 * P],
                                      start=True, stop=False)
                            ins = pe.matmul(dst[rows, at + P:at + 2 * P], f1[:, 1, h, :], et[:, h, 2 * P:3 * P],
                                            start=False, stop=True)
                elif kind == "weigh2":
                    q, t = i // 2, i % 2
                    need(pe, b, "z_copied", 2 * q + 2)
                    for j in range(4):
                        ins = pe.matmul(dst[:, j * P:(j + 1) * P], zt[:, 4 * q + j, t * P:(t + 1) * P], w2_2[:],
                                        start=True, stop=True)
                elif kind == "stack":
                    need(pe, b, "gelu2_done", i // 4 + 1)
                    need(pe, b, "values_out", i // 4 + 1)
                    for j in range(2):
                        for t in range(T):
                            ins = pe.transpose(dst[:, (2 * j + t) * P:(2 * j + t + 1) * P],
                                               of[:, 2 * i + j, t, 0:2 * DH], ident[:])
                elif kind == "x_turn":
                    need(pe, b, "xa_done", 1)
                    for j, src in enumerate((xa, xn)):
                        for t in range(T):
                            ins = pe.transpose(dst[:, (2 * j + t) * P:(2 * j + t + 1) * P], src[:, t, :], ident[:])
                elif kind == "out":
                    if i == 0:
                        pe.wait_ge(once["o_w_split"], 1)
                    need(pe, b, "stack_split", i + 1)
                    for j in range(2):
                        ins = split_product(dst[:, 0:T * P], o_w, of_t, lambda w: w[:, 2 * i + j, :],
                                            lambda x: x[:, i % STACKS, j * T * P:(j + 1) * T * P],
                                            start=(i, j) == (0, 0), stop=(i, j) == (PAIRS - 1, 1))
                elif kind == "out_turn":
                    need(pe, b, "y_copied", 1)
                    for t in range(T):
                        ins = pe.transpose(dst[:, t * P:(t + 1) * P], y_t[:, t * P:(t + 1) * P], ident[:])
                return ins

            pe.wait_ge(once["counters_set"], 1)
            for kind, i in (("gates", 1), ("qm", PAIRS), ("qm", PAIRS + 1), ("scores", H), ("scores", H + 1)):
                product(None, kind, i).then_inc(sem[kind], 1)
            for t in range(T):
                ins = pe.transpose(bank("out_turn", 0)[:, t * P:(t + 1) * P], ident[:], ident[:])
            ins.then_inc(sem["out_turn"], 1)
            with pe.Fori(0, B) as b:
                for kind, i in ORDER:
                    if (kind, i) in slot:
                        free_bank(b, slot[kind, i])
                    product(b, kind, i).then_inc(sem[kind], 1)


_INS = ["x", "gamma_in", "Wq", "Wk", "Wv", "gnn_w", "gnn_b", "lin_w", "lin_b", "Wo", "gamma_out"]
_FFN = ["Wg", "Ws1", "Ws3", "Ws2", "We1", "We3", "We2"]


def kernel(**inputs):
    import numpy as np
    import concourse.bacc as bacc
    from concourse.bass_utils import run_bass_kernel_spmd

    nc = bacc.Bacc("TRN2", target_bir_lowering=False, num_devices=1)
    arrays, args = {}, []
    for name in ["L0_attn_" + n for n in _INS] + ["L0_ffn_" + n for n in _FFN]:
        a = np.ascontiguousarray(inputs[name])
        arrays[f"in_{name}"] = a
        args.append(nc.dram_tensor(f"in_{name}", a.shape, mybir.dt.from_np(a.dtype), kind="ExternalInput").ap())
    out = nc.dram_tensor("out", inputs["L0_attn_x"].shape, F32, kind="ExternalOutput").ap()
    build(nc, *args, out)
    r = run_bass_kernel_spmd(nc, [arrays], core_ids=[0])
    return r.results[0]["out"]
```

```python
from contextlib import ExitStack

import concourse.bass as bass
from concourse import mybir
from concourse.alu_op_type import AluOpType as ALU

F32 = mybir.dt.float32
F32R = mybir.dt.float32r
U32 = mybir.dt.uint32
ACT = mybir.ActivationFunctionType
AX_X = mybir.AxisListType.X

P = 128
T = 2
H, DH = 16, 64
PAIRS = H // 2
E = 9
C = 2
VHW = 2 * DH + 2
BANKS = 8
STACKS = 3
EPS = 1e-5
MASKED = -3.0e38


def product_jobs():
    jobs = []
    up = lambda e: [("gate_up", e), ("up", e)]
    two = lambda kind, n: [(kind, 2 * n), (kind, 2 * n + 1)]
    for s in range(PAIRS):
        if s == 1:
            jobs.append(("vh", s))
        if s >= 1:
            jobs += two("turn", s - 1)
        if s + 1 < PAIRS:
            jobs += two("scores", s + 1)
        if s == 0:
            jobs.append(("out_turn", 0))
        if s != 1:
            jobs.append(("vh", s))
        if s + 2 < PAIRS:
            jobs.append(("qm", s + 2))
        if s != 1:
            jobs += up(max(s - 1, 0))
        if s >= 1:
            jobs += two("layer1", s - 1)
        if s >= 2:
            jobs.append(("down", s - 2))
    jobs += two("turn", PAIRS - 1) + up(7) + two("layer1", PAIRS - 1) + [("down", 6)]
    jobs += two("layer2", 0) + up(8) + two("weigh2", 0) + [("down", 7)]
    jobs += two("layer2", 1) + [("x_turn", 0), ("down", 8)] + two("weigh2", 1)
    stack = lambda p: ("stack", p)
    part = lambda p: ("out", p)
    jobs += [("gates", 1), stack(0), ("qm", PAIRS), stack(1), ("qm", PAIRS + 1), stack(2), part(0), stack(3), part(1)]
    jobs += [("scores", H), stack(4), part(2), stack(5), part(3), stack(6), part(4), stack(7), ("scores", H + 1)]
    jobs += [part(5), part(6), part(7)]
    return jobs


ORDER = product_jobs()
JOBS = [job for job in ORDER if job[0] != "out" or job[1] == 0]
SLOTS = -(-len(JOBS) // BANKS) * BANKS

READ_BY = {
    "gates": "gates_taken", "qm": "qm_split", "vh": "vh_copied", "scores": "scores_masked",
    "turn": "et_copied", "layer1": "layer1_copied", "gate_up": "silu_made", "up": "hidden_made",
    "down": "down_added", "layer2": "z_copied", "weigh2": "weigh2_scaled", "stack": "stack_split",
    "x_turn": "xt_split", "out": "y_copied", "out_turn": "y_normed",
}

AHEAD = {"gates": 1, "gates_taken": 1, "ez_done": 1, "qm": 2, "qm_copied": 2, "qm_split": 2, "scores": 2}
VECTOR_LINKS = 30

PER_SEQ = {
    "gates": 1, "qm": PAIRS, "vh": PAIRS, "scores": H, "turn": H, "layer1": H, "gate_up": E, "up": E,
    "down": E, "layer2": 4, "weigh2": 4, "stack": PAIRS, "x_turn": 1, "out": PAIRS, "out_turn": 1,
    "vh_copied": PAIRS,
    "gates_taken": 1, "ez_done": 1, "qm_copied": PAIRS, "exp_done": 2 * H, "et_copied": H, "layer1_copied": H,
    "tanh_done": E, "gelu1_done": 2, "z_copied": 4, "gelu2_done": 2, "stack_copied": PAIRS,
    "xt_copied": 1, "y_copied": 1,
    "scores_masked": H, "negmax_done": PAIRS, "diag_set": PAIRS, "silu_made": E,
    "hidden_made": E, "down_added": E, "norms_done": 2, "layer1_sum": 2,
    "weigh2_scaled": 4, "layer2_sum": 2, "y_normed": 1, "var_eps": 3, "xa_done": 1, "chain": VECTOR_LINKS, "qm_split": PAIRS,
    "stack_split": PAIRS, "xt_split": 1, "x_taken": 1,
    "v_biased": 2, "values_out": 2, "f1_biased": 2, "rstd_done": 3, "result_done": 1,
    "pool_chain": 3,
    "result_left": 1,
}


def build(nc, x, gamma_in, Wq, Wk, Wv, gnn_w, gnn_b, lin_w, lin_b, Wo, gamma_out,
          Wg, Ws1, Ws3, Ws2, We1, We3, We2, out):
    B = x.shape[0]
    DM = x.shape[2]
    F = C * P
    FE = E * F
    assert x.shape[1] == T * P and DM == P

    with ExitStack() as ctx:
        def sb(name, shape, dt=F32):
            return ctx.enter_context(nc.sbuf_tensor(name, shape, dt))

        def halves(name, shape):
            return sb(name + "_hi", shape, F32R), sb(name + "_lo", shape, F32R)

        def plain(ap):
            return ap.bitcast(F32)

        sem = {n: ctx.enter_context(nc.semaphore(n)) for n in PER_SEQ}
        once = {n: ctx.enter_context(nc.semaphore(n)) for n in (
            "ld_x0", "x_loaded", "ld_q", "ld_k", "ld_v", "ld_gamma", "ld_g", "ld_o", "ld_e", "ld_raw", "pool_setup", "setup_product",
            "act_setup", "dve_setup", "rounded", "o_w_rounded", "vh_w_split", "wg_split", "shared_split", "ffn_w_split", "o_w_split", "wo_summed",
            "counters_set", "stored", "first_var_eps", "first_rstd", "first_xa", "dve_chain")}

        def need(eng, b, name, count):
            assert 0 <= count <= PER_SEQ[name] + AHEAD.get(name, 0), (name, count)
            if b is None:
                eng.wait_ge(sem[name], count - PER_SEQ[name] + 1)
            else:
                eng.wait_ge(sem[name], b * PER_SEQ[name] + count + 1)

        psum = ctx.enter_context(nc.psum_tensor("psum", [P, BANKS, 512], F32))
        slot = {job: n for n, job in enumerate(JOBS)}

        def bank(kind, i):
            if (kind, i) not in slot:
                i += PER_SEQ[kind]
            return psum[:, slot[kind, i] % BANKS, :]

        ident = sb("ident", [P, P])
        mask1 = sb("mask1", [P, 2 * P])
        mask0 = mask1[:, P:2 * P]
        rank = sb("rank", [P, 8])
        minus_half = sb("minus_half", [P, T])
        gamma_col = sb("gamma_col", [P, 1])
        gamma_out_row = sb("gamma_out_row", [P, P])
        b1_row = sb("b1_row", [P, DH])
        b2_row = sb("b2_row", [P, DH])
        lin_b_col = sb("lin_b_col", [DH, 1])
        w2_2 = sb("w2_2", [P, P])
        m_w = halves("m_w", [P, H, P])
        vh_w = halves("vh_w", [P, H, 2 * DH])
        o_w = halves("o_w", [P, H, P])
        out_bias = sb("out_bias", [P, 1])
        wg = halves("wg", [P, 8])
        w_gate = halves("w_gate", [P, E, F])
        w_up = halves("w_up", [P, E, F])
        w_down = sb("w_down", [P, E, C, P])

        x_in = sb("x_in", [P, T, P])
        xa_t0 = sb("xa_t0", [P, P])
        xa_t = halves("xa_t", [P, T * P])
        xn_t = halves("xn_t", [P, T * P])
        stats = sb("stats", [P, T, 6])
        mv = sb("mv", [P, T, 2])
        var_eps = sb("var_eps", [P, T])
        rstd = sb("rstd", [P, T])
        qm1 = halves("qm1", [P, 2, 2, P])
        vh = sb("vh", [P, T, H, VHW])
        work = sb("work", [P, PAIRS * T * P])
        ex = work[:, 0:4 * 3 * P].rearrange("p (h k j) -> p h k j", h=4, k=3)
        qm0 = work[:, 4 * 3 * P:4 * 4 * P].rearrange("p (q a n) -> p q a n", q=2, a=2)
        mx = sb("mx", [P, H, T])
        negmax = sb("negmax", [P, H, T])
        D = sb("D", [P, H, T])
        et = sb("et", [P, H, 3 * P])
        spare = et[:].rearrange("p h n -> p (h n)")
        hd = H * DH
        wt = spare[:, 0:3 * hd].rearrange("p (k q d) -> p k q d", k=3, q=PAIRS)
        wq, wk, wv = (spare[:, n * hd:(n + 1) * hd] for n in (3, 4, 5))
        l1 = sb("l1", [P, H, T, VHW])
        rD = sb("rD", [P, H, T])
        rG = sb("rG", [P, H, T])
        kV = sb("kV", [P, H, T])
        h1 = sb("h1", [P, T, H, DH])
        h2 = h1
        f1 = sb("f1", [P, T, H, DH])
        zt = work[:, 0:PAIRS * T * P].rearrange("p (q n) -> p q n", q=PAIRS)
        of = l1
        vo = vh[:, :, :, DH:2 * DH]
        of_t = halves("of_t", [P, STACKS, 2 * T * P])
        ys = sb("ys", [P, 2, T * P])
        y_t = ys[:, 0, :]
        xa = y_t.rearrange("p (t d) -> p t d", t=T)
        yn = ys[:, 1, :].rearrange("p (t d) -> p t d", t=T)
        xn = yn
        hid = sb("hid", [P, 2, C * T * P])
        s_raw = hid[:, 0, :].rearrange("p (k f) -> p k f", k=2)
        wg_raw = hid[:, 1, 0:8]
        g_raw = h1[:].rearrange("p t h d -> p (t h d)").rearrange("p (e f) -> p e f", f=F)
        u_raw = f1[:].rearrange("p t h d -> p (t h d)").rearrange("p (e f) -> p e f", f=F)
        wo_raw = l1[:].rearrange("p h t d -> p (h t d)")[0:DH, 0:H * P].rearrange("p (h n) -> p h n", h=H)
        ones, w1_2 = work[:, 0:P], work[:, P:2 * P]
        lin_sb, lin_t = (work[0:DH, n * P:n * P + DH] for n in (2, 3))
        wo_part = work[0:DH, 4 * P:12 * P].rearrange("p (h n) -> p h n", n=P)
        ffn = sb("ffn", [P, T, P])
        z_exp = sb("z_exp", [P, T, 8])
        ez = sb("ez", [P, T, 8])
        gates = sb("gates_sb", [P, T, 8])
        gw = sb("gw", [P, 8, T, 8])
        gv = sb("gv", [P, 6, T])
        w_exp = sb("w_exp", [P, T, 8])
        carrier = sb("carrier", [P, 48])

        x_dram = x.rearrange("b (t p) d -> b p t d", p=P)
        out_dram = out.rearrange("b (t p) d -> b p t d", p=P)

        block = ctx.enter_context(nc.Block())

        def bc(ap, n):
            return ap.unsqueeze(len(ap.shape)).to_broadcast(list(ap.shape) + [n])

        def heads_t(ap):
            return ap.rearrange("p h t -> p t h")

        LOADS = dict(ld_x0=1, ld_q=1, ld_k=1, ld_v=6, ld_gamma=1, ld_g=3, ld_o=3, ld_e=3, ld_raw=4)

        def loaded(eng, name):
            eng.wait_ge(once[name], 16 * LOADS[name])

        @block.sync
        def _(sp):
            sp.dma_start(x_in[:], x_dram[0]).then_inc(once["ld_x0"], 16)
            sp.dma_start(wq, Wq).then_inc(once["ld_q"], 16)
            sp.dma_start(wv, Wv).then_inc(once["ld_v"], 16)
            sp.dma_start(wg_raw, Wg).then_inc(once["ld_v"], 16)
            sp.wait_ge(once["pool_setup"], 2)
            for n in range(2):
                for k, w in ((0, w1_2), (1, w2_2)):
                    sp.dma_start(w[n * DH:(n + 1) * DH, n * DH:(n + 1) * DH], gnn_w[k]).then_inc(once["ld_v"], 16)
            sp.dma_start(wo_raw, Wo.rearrange("(h p) n -> p h n", p=DH)).then_inc(once["ld_o"], 16)
            sp.dma_start(lin_sb, lin_w).then_inc(once["ld_o"], 16)
            sp.dma_start(lin_b_col[:], lin_b.rearrange("(p o) -> p o", o=1)).then_inc(once["ld_o"], 16)
            sp.dma_start(g_raw, We1.rearrange("e d f -> d e f")).then_inc(once["ld_raw"], 16)
            sp.dma_start(s_raw[:, 0, :], Ws1).then_inc(once["ld_raw"], 16)
            sp.dma_start(s_raw[:, 1, :], Ws3).then_inc(once["ld_raw"], 16)
            sp.dma_start(u_raw, We3.rearrange("e d f -> d e f")).then_inc(once["ld_raw"], 16)
            sp.dma_start(b1_row[:], gnn_b[0].partition_broadcast(P)).then_inc(once["ld_g"], 16)
            sp.dma_start(b2_row[:], gnn_b[1].partition_broadcast(P)).then_inc(once["ld_g"], 16)
            sp.dma_start(gamma_out_row[:], gamma_out.partition_broadcast(P)).then_inc(once["ld_g"], 16)
            sp.dma_start(w_down[:, 0], Ws2.rearrange("(c p) d -> p c d", p=P)).then_inc(once["ld_e"], 16)
            sp.dma_start(w_down[:, 1:5], We2[0:4].rearrange("e (c p) d -> p e c d", p=P)).then_inc(once["ld_e"], 16)
            sp.dma_start(w_down[:, 5:9], We2[4:8].rearrange("e (c p) d -> p e c d", p=P)).then_inc(once["ld_e"], 16)
            sp.wait_ge(once["counters_set"], 1)
            with sp.Fori(0, B) as b:
                need(sp, b, "result_done", 1)
                sp.dma_start(out_dram[(b + B - 1) % B], yn).then_inc(once["stored"], 16)
                sp.wait_ge(once["stored"], b * 16 + 16)
                sp.sem_inc(sem["result_left"], 1)
                need(sp, b, "x_taken", 1)
                sp.dma_start(x_in[:], x_dram[(b + 1) % B]).then_inc(once["x_loaded"], 16)
            need(sp, B, "result_done", 1)
            sp.dma_start(out_dram[B - 1], yn).then_inc(once["stored"], 16)
            sp.wait_ge(once["stored"], 16 * (B + 1))
            sp.wait_ge(once["x_loaded"], 16 * B)

        SETUP = (["w_turn"] * 6 + ["x_turn"] + ["lin_turn"] + ["m"] * 4 + ["vw1"] * 2 + ["lin_wo"] * 4 + ["bias"])
        first = {k: SETUP.index(k) for k in SETUP}
        SHIFT = 6
        setup_psum = lambda n: psum[:, (n + SHIFT) % BANKS, :]

        def by_act(n):
            return SETUP[n] != "w_turn" or (n - first["w_turn"]) % 2 == 0

        def by_dve(n):
            return not by_act(n) or SETUP[n] not in ("w_turn", "lin_turn", "bias")

        def emptied(eng, n):
            eng.wait_ge(once["act_setup"], sum(map(by_act, range(n + 1))))
            if any(map(by_dve, range(n + 1))):
                eng.wait_ge(once["dve_setup"], sum(map(by_dve, range(n + 1))))

        def setup_targets(n):
            src = setup_psum(n)
            kind, k = SETUP[n], n - first[SETUP[n]]
            by4 = src.rearrange("p (q d) -> p q d", q=4)
            if kind == "w_turn":
                return [(wt.rearrange("p k q d -> p (k q) d")[:, 4 * k:4 * k + 4, :], None, by4, 1.0)]
            if kind == "m":
                at = slice(8 * (k // 2) + k % 2, 8 * (k // 2) + 8, 2)
                return [(m_w[0][:, at, :], m_w[1][:, at, :], by4, DH ** -0.5)]
            if kind == "vw1":
                hi, lo = (w[:, 8 * k:8 * k + 8, DH:2 * DH] for w in vh_w)
                return [(hi, lo, src.rearrange("p (q d) -> p q d", q=8), 1.0)]
            if kind == "lin_turn":
                return [(lin_t, None, src[0:DH, 0:DH], 1.0)]
            if kind == "lin_wo":
                hi, lo = (w[DH:P, 4 * k:4 * k + 4, :] for w in o_w)
                return [(hi, lo, by4[DH:P], 1.0)]
            return [(out_bias[:], None, src[:, 0:1], 1.0)]

        def turned_by_act(src):
            nc.scalar.activation(xa_t[0][:], src[:, 0:T * P], ACT.Copy, scale=gamma_col[:, 0:1])
            return nc.scalar.copy(xn_t[0][:], src[:, T * P:2 * T * P])

        def turned_by_dve(src):
            nc.vector.scalar_tensor_tensor(out=xa_t[1][:], in0=src[:, 0:T * P], scalar=gamma_col[:, 0:1],
                                           in1=plain(xa_t[0][:]), op0=ALU.mult, op1=ALU.subtract)
            nc.vector.tensor_tensor(xn_t[1][:], src[:, T * P:2 * T * P], plain(xn_t[0][:]), ALU.subtract)
            return nc.vector.tensor_scalar(xa_t0[:], src[:, 0:P], gamma_col[:, 0:1], None, ALU.mult)

        ROUNDED = {
            "vh_w": ([w[:, :, 0:DH] for w in vh_w], wv.rearrange("p (h d) -> p h d", h=H), "ld_v"),
            "wg": ([w[:] for w in wg], wg_raw, "ld_v"),
            "gate0": ([w[:, 0, :] for w in w_gate], s_raw[:, 0, :], "ld_raw"),
            "up0": ([w[:, 0, :] for w in w_up], s_raw[:, 1, :], "ld_raw"),
            "gate": ([w[:, 1:E, :] for w in w_gate], g_raw, "ld_raw"),
            "up": ([w[:, 1:E, :] for w in w_up], u_raw, "ld_raw"),
            "o_w": ([w[0:DH] for w in o_w], wo_raw, "ld_o"),
        }

        def upper_half(act, *names):
            for name in names:
                (hi, _), raw, load = ROUNDED[name]
                loaded(act, load)
                nc.scalar.copy(hi, raw).then_inc(once["rounded"], 1)

        def lower_half(engine, eng, name):
            (hi, lo), raw, _ = ROUNDED[name]
            if name != "o_w":
                eng.wait_ge(once["rounded"], list(ROUNDED).index(name) + 1)
            return engine.tensor_tensor(lo, raw, plain(hi), ALU.subtract)

        @block.gpsimd
        def _(pool):
            pool.memset(w1_2, 0.0).then_inc(once["pool_setup"], 1)
            pool.memset(w2_2[:], 0.0).then_inc(once["pool_setup"], 1)
            pool.memset(minus_half[:], -0.5)
            pool.memset(ffn[:], 0.0)
            pool.memset(mask1[:], 0.0)
            pool.memset(vh[:, :, :, 2 * DH:VHW], 1.0)
            pool.memset(ones, 1.0).then_inc(once["pool_setup"], 1)
            pool.iota(rank[:], pattern=[[-1, 8]], base=8, channel_multiplier=0,
                      allow_small_or_imprecise_dtypes=True)
            pool.wait_ge(once["pool_setup"], 3)
            pool.affine_select(out=ident[:], in_=ones, compare_op=ALU.is_equal, fill=0.0, base=0,
                               pattern=[[-1, P]], channel_multiplier=1)
            pool.affine_select(out=mask1[:, P:2 * P], in_=mask1[:, P:2 * P], compare_op=ALU.is_ge,
                               fill=MASKED, base=0, pattern=[[-1, P]],
                               channel_multiplier=1).then_inc(once["pool_setup"], 1)
            for n in range(2):
                pool.wait_ge(once["first_var_eps"], n + 1)
                pool.tensor_tensor(rstd[:], var_eps[:], minus_half[:], ALU.pow).then_inc(once["first_rstd"], 1)
            for n in sem:
                pool.sem_inc(sem[n], 1)
            pool.sem_inc(once["counters_set"], 1)
            loaded(pool, "ld_o")
            for n, left in enumerate((8, 4, 2, 1)):
                if n:
                    pool.wait_ge(once["wo_summed"], n)
                rest = wo_part if n else wo_raw
                pool.tensor_tensor(wo_part[:, 0:left, :], rest[:, 0:left, :], rest[:, left:2 * left, :],
                                   ALU.add).then_inc(once["wo_summed"], 1)
                if left == 4:
                    lower_half(nc.gpsimd, pool, "wg").then_inc(once["wg_split"], 1)
                    lower_half(nc.gpsimd, pool, "vh_w").then_inc(once["vh_w_split"], 1)
            lower_half(nc.gpsimd, pool, "gate0")
            lower_half(nc.gpsimd, pool, "up0").then_inc(once["shared_split"], 1)
            pool.wait_ge(once["o_w_rounded"], 1)
            lower_half(nc.gpsimd, pool, "o_w").then_inc(once["o_w_split"], 1)
            lower_half(nc.gpsimd, pool, "up").then_inc(once["ffn_w_split"], 1)
            loaded(pool, "ld_g")

            def rstd_of(b, n):
                need(pool, b, "var_eps", n + 1)
                pool.tensor_tensor(rstd[:], var_eps[:], minus_half[:], ALU.pow).then_inc(sem["rstd_done"], 1)

            pool.wait_ge(once["counters_set"], 1)
            def finish(b):
                rstd_of(b, 0)
                need(pool, b, "down_added", 0)
                need(pool, b, "y_normed", 1)
                pool.tensor_tensor(yn, yn, gamma_out_row[:].unsqueeze(1).to_broadcast([P, T, P]),
                                   ALU.mult).then_inc(sem["pool_chain"], 1)
                need(pool, b, "pool_chain", 1)
                pool.tensor_tensor(yn, yn, ffn[:], ALU.add).then_inc(sem["result_done"], 1)

            with pool.Fori(0, B) as b:
                finish(b)
                def bias_v(hf):
                    hs = slice(hf * PAIRS, (hf + 1) * PAIRS)
                    need(pool, b, "vh_copied", 4 * hf + 4)
                    if hf == 0:
                        need(pool, b, "gelu2_done", 0)
                    pool.tensor_tensor(h1[:, :, hs, :], vh[:, :, hs, 0:DH],
                                       b1_row[:].unsqueeze(1).unsqueeze(1).to_broadcast([P, T, PAIRS, DH]),
                                       ALU.add).then_inc(sem["v_biased"], 1)

                def bias_f1(hf):
                    hs = slice(hf * PAIRS, (hf + 1) * PAIRS)
                    need(pool, b, "gelu1_done", hf + 1)
                    pool.tensor_tensor(h2[:, :, hs, :], f1[:, :, hs, :],
                                       b2_row[:].unsqueeze(1).unsqueeze(1).to_broadcast([P, T, PAIRS, DH]),
                                       ALU.add).then_inc(sem["f1_biased"], 1)

                bias_v(0)
                rstd_of(b, 1)
                rstd_of(b, 2)
                bias_v(1)
                for hf in range(2):
                    hs = slice(hf * PAIRS, (hf + 1) * PAIRS)
                    need(pool, b, "norms_done", hf + 1)
                    pool.tensor_tensor(vo[:, :, hs], vh[:, :, hs, 0:DH], bc(heads_t(kV[:, hs]), DH), ALU.mult)
                    values = of[:, hs, :, 0:DH].rearrange("p h t d -> p t h d")
                    pool.tensor_tensor(values, values,
                                       bc(heads_t(rD[:, hs]), DH), ALU.mult).then_inc(sem["pool_chain"], 1)
                    need(pool, b, "pool_chain", hf + 2)
                    pool.tensor_tensor(values, values, vo[:, :, hs], ALU.add).then_inc(sem["values_out"], 1)
                    if hf == 0:
                        bias_f1(0)
                bias_f1(1)
            finish(B)

        @block.scalar
        def _(act):
            act.dma_start(gamma_col[:], gamma_in.rearrange("(p o) -> p o", o=1)).then_inc(once["ld_gamma"], 16)
            act.dma_start(wk, Wk).then_inc(once["ld_k"], 16)
            for n in range(len(SETUP)):
                if n == first["x_turn"]:
                    loaded(act, "ld_gamma")
                if n == first["m"]:
                    upper_half(act, "vh_w", "wg")
                if n == first["lin_wo"]:
                    upper_half(act, "gate0", "up0")
                if by_act(n):
                    act.wait_ge(once["setup_product"], n + 1)
                    if SETUP[n] == "x_turn":
                        ins = turned_by_act(setup_psum(n))
                    else:
                        for whole, _, src, scale in setup_targets(n):
                            ins = nc.scalar.activation(whole, src, ACT.Copy, scale=scale)
                    ins.then_inc(once["act_setup"], 1)
            upper_half(act, "gate")

            def read(b, kind, n):
                need(act, b, kind, n + 1)
                return bank(kind, 0 if kind == "out" else n)

            def copy_qm(b, p):
                need(act, b, "qm", p + 1)
                src = bank("qm", p).rearrange("p (a n) -> p a n", a=2)
                if b is not None:
                    need(act, b, "scores", 2 * p - 2)
                nc.scalar.copy(qm0[:, p % 2], src[:, :, 0:P])
                nc.scalar.copy(qm1[0][:, p % 2], src[:, :, P:2 * P]).then_inc(sem["qm_copied"], 1)

            def take_gates(src):
                nc.scalar.copy(z_exp[:], src[:, 0:T * 8].rearrange("p (t e) -> p t e", t=T)
                               ).then_inc(sem["gates_taken"], 1)

            def exp_gates(b):
                need(act, b, "gates_taken", 2)
                nc.scalar.activation(ez[:], z_exp[:], ACT.Exp, scale=-1.0).then_inc(sem["ez_done"], 1)

            def exps(b, h):
                need(act, b, "negmax_done", h // 2 + 1)
                for t in range(T):
                    blocks = slice(0, 1) if t == 0 else slice(1, 3)
                    e = ex[:, h % 4, blocks, :].rearrange("p k j -> p (k j)")
                    nc.scalar.activation(e, e, ACT.Exp, bias=negmax[:, h, t:t + 1], scale=1.0,
                                         accum_out=D[:, h, t:t + 1]).then_inc(sem["exp_done"], 1)

            def copy_et(b, h):
                src = read(b, "turn", h)
                nc.scalar.copy(et[:, h, :], src[:, 0:3 * P]).then_inc(sem["et_copied"], 1)

            def copy_vh(b, n):
                q, t = n // 2, n % 2
                src = read(b, "vh", n)
                nc.scalar.copy(vh[:, t, 4 * q:4 * q + 4, 0:2 * DH], src.rearrange("p (h d) -> p h d", h=4)
                               ).then_inc(sem["vh_copied"], 1)

            def copy_l1(b, h):
                src = read(b, "layer1", h)
                if h == 0:
                    act.wait_ge(once["o_w_split"], 1)
                nc.scalar.copy(l1[:, h, :, :], src[:, 0:T * VHW].rearrange("p (t d) -> p t d", t=T)
                               ).then_inc(sem["layer1_copied"], 1)

            def tanh(b, e):
                src = read(b, "gate_up", e)
                need(act, b, "down", max(e - 1, 0))
                nc.scalar.activation(hid[:, e % 2, :], src, ACT.Tanh, scale=0.5).then_inc(sem["tanh_done"], 1)

            def gelu1(b, hf):
                hs = slice(hf * PAIRS, (hf + 1) * PAIRS)
                need(act, b, "layer1_sum", hf + 1)
                nc.scalar.activation(f1[:, :, hs, :], h1[:, :, hs, :], ACT.Gelu).then_inc(sem["gelu1_done"], 1)

            def gelu2(b, hf):
                hs = slice(hf * PAIRS, (hf + 1) * PAIRS)
                need(act, b, "layer2_sum", hf + 1)
                nc.scalar.activation(of[:, hs, :, DH:2 * DH].rearrange("p h t d -> p t h d"), h2[:, :, hs, :],
                                     ACT.Gelu).then_inc(sem["gelu2_done"], 1)

            def copy_z(b, g):
                src = read(b, "layer2", g)
                nc.scalar.copy(zt[:, 2 * g:2 * g + 2, :].rearrange("p q n -> p (q n)"), src
                               ).then_inc(sem["z_copied"], 1)

            def copy_stack(b, p):
                src = read(b, "stack", p)
                if p >= STACKS:
                    need(act, b, "out", p - STACKS + 1)
                nc.scalar.copy(of_t[0][:, p % STACKS, :], src).then_inc(sem["stack_copied"], 1)

            act.wait_ge(once["counters_set"], 1)
            need(act, None, "gates", 2)
            take_gates(bank("gates", 1))
            exp_gates(None)
            copy_qm(None, PAIRS)
            copy_qm(None, PAIRS + 1)
            upper_half(act, "up")
            with act.Fori(0, B) as b:
                need(act, b, "norms_done", 0)
                need(act, b, "values_out", 0)
                exps(b, 0)
                exps(b, 1)
                for s in range(PAIRS):
                    if s == 1:
                        copy_vh(b, s)
                    if s >= 1:
                        copy_et(b, 2 * s - 2)
                        copy_et(b, 2 * s - 1)
                    if s != 1:
                        copy_vh(b, s)
                    if s + 2 < PAIRS:
                        copy_qm(b, s + 2)
                    if s + 1 < PAIRS:
                        exps(b, 2 * s + 2)
                    if s != 1:
                        tanh(b, max(s - 1, 0))
                    if s + 1 < PAIRS:
                        exps(b, 2 * s + 3)
                    if s >= 1:
                        copy_l1(b, 2 * s - 2)
                        copy_l1(b, 2 * s - 1)
                copy_et(b, H - 2)
                copy_et(b, H - 1)
                tanh(b, 7)
                gelu1(b, 0)
                copy_l1(b, H - 2)
                copy_l1(b, H - 1)
                copy_z(b, 0)
                copy_z(b, 1)
                tanh(b, 8)
                gelu1(b, 1)
                copy_z(b, 2)
                copy_z(b, 3)
                turned_by_act(read(b, "x_turn", 0)).then_inc(sem["xt_copied"], 1)
                gelu2(b, 0)
                take_gates(read(b, "gates", 1))
                copy_stack(b, 0)
                copy_qm(b, PAIRS)
                copy_stack(b, 1)
                copy_qm(b, PAIRS + 1)
                gelu2(b, 1)
                for p in range(2, 8):
                    copy_stack(b, p)
                exp_gates(b)
                src = read(b, "out", PAIRS - 1)
                nc.scalar.activation(y_t, src[:, 0:T * P], ACT.Identity, bias=out_bias[:, 0:1]
                                     ).then_inc(sem["y_copied"], 1)

        @block.vector
        def _(dve):
            V = nc.vector

            carried = [0]

            def carry_wait():
                carried[0] += 1
                return V.memset(carrier[:, carried[0] - 1:carried[0]], 0.0)

            def mean_var(n, src, link):
                for t in range(T):
                    ins = V.bn_stats(stats[:, t, :], src(t))
                link(ins)
                carry_wait()
                for t in range(T):
                    ins = V.bn_aggr(mv[:, t, :], stats[:, t, :])
                link(ins)
                return V.tensor_scalar(var_eps[:], mv[:, :, 1], EPS, None, ALU.add)

            def normed(dst, src):
                for t in range(T):
                    ins = V.tensor_scalar(dst(t), src(t), mv[:, t, 0:1], rstd[:, t:t + 1], ALU.subtract, ALU.mult)
                return ins

            links = [0]

            def link_once(ins):
                links[0] += 1
                ins.then_inc(once["dve_chain"], 1)
                dve.wait_ge(once["dve_chain"], links[0])

            loaded(dve, "ld_x0")
            mean_var(0, lambda t: x_in[:, t, :], link_once).then_inc(once["first_var_eps"], 1)
            dve.wait_ge(once["first_rstd"], 1)
            link_once(normed(lambda t: xn[:, t, :], lambda t: x_in[:, t, :]))
            mean_var(1, lambda t: xn[:, t, :], link_once).then_inc(once["first_var_eps"], 1)
            dve.wait_ge(once["first_rstd"], 2)
            normed(lambda t: xa[:, t, :], lambda t: xn[:, t, :]).then_inc(once["first_xa"], 1)
            dve.wait_ge(once["pool_setup"], 4)
            for n in range(len(SETUP)):
                if n == first["x_turn"]:
                    loaded(dve, "ld_gamma")
                if by_dve(n):
                    dve.wait_ge(once["setup_product"], n + 1)
                    if by_act(n):
                        emptied_by_act = sum(map(by_act, range(n + 1)))
                        dve.wait_ge(once["act_setup"], emptied_by_act)
                    if SETUP[n] == "x_turn":
                        ins = turned_by_dve(setup_psum(n))
                    else:
                        for hi, lo, src, scale in setup_targets(n):
                            if lo is None:
                                ins = V.tensor_copy(hi, src)
                            else:
                                ins = V.scalar_tensor_tensor(out=lo, in0=src, scalar=scale, in1=plain(hi),
                                                             op0=ALU.mult, op1=ALU.subtract)
                    ins.then_inc(once["dve_setup"], 1)
            V.tensor_copy(ROUNDED["o_w"][0][0], wo_raw).then_inc(once["o_w_rounded"], 1)

            def read(b, kind, n):
                need(dve, b, kind, n + 1)
                return bank(kind, n)

            def mask_scores(b, p):
                for h in (2 * p, 2 * p + 1):
                    src = read(b, "scores", h)
                    need(dve, b, "turn", max(h - 3, 0))
                    carry_wait()
                    V.tensor_tensor_reduce(ex[:, h % 4, 0, :], src[:, 0:P], mask0, 1.0, MASKED,
                                           ALU.add, ALU.max, mx[:, h, 0:1])
                    V.tensor_tensor_reduce(ex[:, h % 4, 1:3, :].rearrange("p k j -> p (k j)"), src[:, P:3 * P], mask1[:], 1.0, MASKED,
                                           ALU.add, ALU.max, mx[:, h, 1:2]).then_inc(sem["scores_masked"], 1)
                need(dve, b, "scores_masked", 2 * p + 2)
                V.tensor_scalar(negmax[:, 2 * p:2 * p + 2, :], mx[:, 2 * p:2 * p + 2, :], -1.0, None,
                                ALU.mult).then_inc(sem["negmax_done"], 1)

            def split_qm(b, p):
                need(dve, b, "qm_copied", p + 1)
                src = bank("qm", p).rearrange("p (a n) -> p a n", a=2)
                V.tensor_tensor(qm1[1][:, p % 2], src[:, :, P:2 * P], plain(qm1[0][:, p % 2]),
                                ALU.subtract).then_inc(sem["qm_split"], 1)

            def split_stack(b, p):
                need(dve, b, "stack_copied", p + 1)
                V.tensor_tensor(of_t[1][:, p % STACKS, :], bank("stack", p), plain(of_t[0][:, p % STACKS, :]),
                                ALU.subtract).then_inc(sem["stack_split"], 1)

            def set_diagonal(b, p):
                need(dve, b, "exp_done", 4 * p + 4)
                carry_wait()
                r = 2 * (p % 2)
                V.copy_predicated(ex[:, r:r + 2, 0:3:2, :],
                                  ident[:].bitcast(U32).unsqueeze(1).unsqueeze(1).to_broadcast([P, 2, 2, P]),
                                  bc(D[:, 2 * p:2 * p + 2, :], P)).then_inc(sem["diag_set"], 1)

            def norms(b, hf, link):
                hs = slice(hf * PAIRS, (hf + 1) * PAIRS)
                need(dve, b, "layer1_copied", PAIRS * (hf + 1))
                V.reciprocal(rG[:, hs], l1[:, hs, :, 2 * DH])
                link(V.reciprocal(rD[:, hs], D[:, hs]))
                link(V.tensor_tensor(kV[:, hs], l1[:, hs, :, 2 * DH], rD[:, hs], ALU.mult))
                V.tensor_scalar(kV[:, hs], kV[:, hs], -1.0, 1.0, ALU.mult, ALU.add).then_inc(sem["norms_done"], 1)

            def scale_layer1(b, hf, link):
                hs = slice(hf * PAIRS, (hf + 1) * PAIRS)
                weighed = l1[:, hs, :, DH:2 * DH].rearrange("p h t d -> p t h d")
                link(V.tensor_tensor(weighed, weighed, bc(heads_t(rG[:, hs]), DH), ALU.mult))
                need(dve, b, "v_biased", hf + 1)
                V.tensor_tensor(h1[:, :, hs, :], weighed, h1[:, :, hs, :], ALU.add).then_inc(sem["layer1_sum"], 1)

            def choose(b, part, link):
                need(dve, b, "ez_done", 1)
                g, m, s1, o1, g2, s2, o2 = (gw[:, i] for i in range(7))
                v1, v2, p1, p2, den, rden = (gv[:, i] for i in range(6))
                ranks = rank[:].unsqueeze(1).to_broadcast([P, T, 8])
                if part == 0:
                    link(V.tensor_scalar(g, ez[:], 1.0, None, ALU.add))
                    link(V.reciprocal(gates[:], g))
                    link(V.tensor_reduce(v1, gates[:], AX_X, ALU.max))
                    link(V.tensor_tensor(m, gates[:], bc(v1, 8), ALU.is_equal))
                    link(V.tensor_tensor(s1, m, ranks, ALU.mult))
                    link(V.tensor_reduce(p1, s1, AX_X, ALU.max))
                    link(V.tensor_tensor(o1, s1, bc(p1, 8), ALU.is_equal))
                elif part == 1:
                    link(V.scalar_tensor_tensor(out=g2, in0=o1, scalar=-4.0, in1=gates[:], op0=ALU.mult, op1=ALU.add))
                    link(V.tensor_reduce(v2, g2, AX_X, ALU.max))
                    link(V.tensor_tensor(m, g2, bc(v2, 8), ALU.is_equal))
                    link(V.tensor_tensor(s2, m, ranks, ALU.mult))
                    link(V.tensor_reduce(p2, s2, AX_X, ALU.max))
                    link(V.tensor_tensor(o2, s2, bc(p2, 8), ALU.is_equal))
                else:
                    V.tensor_tensor(den, v1, v2, ALU.add)
                    link(V.tensor_tensor(m, o1, o2, ALU.add))
                    V.reciprocal(rden, den)
                    link(V.tensor_tensor(s2, m, gates[:], ALU.mult))
                    link(V.tensor_tensor(s1, s2, bc(rden, 8), ALU.mult))
                    link(V.tensor_scalar(w_exp[:], s1, 0.5 / 3.0, None, ALU.mult))

            def hidden(b, e):
                g = bank("gate_up", e)
                need(dve, b, "tanh_done", e + 1)
                V.scalar_tensor_tensor(out=hid[:, e % 2, :], in0=hid[:, e % 2, :], scalar=1.0, in1=g,
                                       op0=ALU.add, op1=ALU.mult).then_inc(sem["silu_made"], 1)
                u = read(b, "up", e)
                need(dve, b, "silu_made", e + 1)
                V.tensor_tensor(hid[:, e % 2, :], hid[:, e % 2, :], u, ALU.mult).then_inc(sem["hidden_made"], 1)

            def add_down(b, e):
                src = read(b, "down", e)
                if e == 0:
                    need(dve, b, "result_done", 1)
                    V.scalar_tensor_tensor(out=ffn[:], in0=src[:, 0:T * P].rearrange("p (t d) -> p t d", t=T),
                                           scalar=0.5 / 3.0, in1=x_in[:], op0=ALU.mult,
                                           op1=ALU.add).then_inc(sem["down_added"], 1)
                    need(dve, b, "down_added", 1)
                    carry_wait().then_inc(sem["x_taken"], 1)
                    return
                need(dve, b, "down_added", e)
                for t in range(T):
                    ins = V.scalar_tensor_tensor(out=ffn[:, t, :], in0=src[:, t * P:(t + 1) * P],
                                                 scalar=w_exp[:, t, e - 1:e], in1=ffn[:, t, :],
                                                 op0=ALU.mult, op1=ALU.add)
                ins.then_inc(sem["down_added"], 1)

            def scale_weigh2(b, n):
                q, t = n // 2, n % 2
                hs = slice(q * PAIRS, (q + 1) * PAIRS)
                src = read(b, "weigh2", n)
                need(dve, b, "f1_biased", q + 1)
                V.tensor_tensor(f1[:, t, hs, :], src.rearrange("p (h d) -> p h d", h=PAIRS),
                                bc(rG[:, hs, t], DH), ALU.mult).then_inc(sem["weigh2_scaled"], 1)

            def sum_layer2(b, hf):
                hs = slice(hf * PAIRS, (hf + 1) * PAIRS)
                need(dve, b, "weigh2_scaled", 2 * hf + 2)
                V.tensor_tensor(h2[:, :, hs, :], h2[:, :, hs, :], f1[:, :, hs, :],
                                ALU.add).then_inc(sem["layer2_sum"], 1)

            dve.wait_ge(once["counters_set"], 1)
            split_qm(None, PAIRS)
            split_qm(None, PAIRS + 1)
            lower_half(V, dve, "gate").then_inc(once["ffn_w_split"], 1)
            count = [0]

            def linker(b):
                def link(ins):
                    count[0] += 1
                    ins.then_inc(sem["chain"], 1)
                    need(dve, b, "chain", count[0])
                return link

            y = bank("out_turn", 0)

            def finish_stats(b, link):
                need(dve, b, "out_turn", 1)
                mean_var(2, lambda t: y[:, t * P:(t + 1) * P], link).then_inc(sem["var_eps"], 1)

            def finish_norm(b):
                need(dve, b, "rstd_done", 1)
                normed(lambda t: yn[:, t, :], lambda t: y[:, t * P:(t + 1) * P]).then_inc(sem["y_normed"], 1)

            with dve.Fori(0, B) as b:
                link = linker(b)
                mask_scores(b, 0)
                for s in range(PAIRS):
                    if s >= 1:
                        set_diagonal(b, s)
                    if s >= 3:
                        add_down(b, s - 3)
                    if s + 1 < PAIRS:
                        mask_scores(b, s + 1)
                    if s == 0:
                        finish_stats(b, link)
                        set_diagonal(b, s)
                    if s == 6:
                        norms(b, 0, link)
                    if s + 2 < PAIRS:
                        split_qm(b, s + 2)
                    if s == 0:
                        finish_norm(b)
                    if s != 1:
                        hidden(b, max(s - 1, 0))
                    if 1 <= s <= 3:
                        choose(b, s - 1, link)
                    if s == 5:
                        dve.wait_ge(once["x_loaded"], b * 16 + 16)
                        mean_var(0, lambda t: x_in[:, t, :], link).then_inc(sem["var_eps"], 1)
                    if s == 6:
                        need(dve, b, "rstd_done", 2)
                        need(dve, b, "result_left", 1)
                        link(normed(lambda t: xn[:, t, :], lambda t: x_in[:, t, :]))
                        mean_var(1, lambda t: xn[:, t, :], link).then_inc(sem["var_eps"], 1)
                    if s == 7:
                        scale_layer1(b, 0, link)
                        need(dve, b, "rstd_done", 3)
                        normed(lambda t: xa[:, t, :], lambda t: xn[:, t, :]).then_inc(sem["xa_done"], 1)
                add_down(b, 5)
                hidden(b, 7)
                norms(b, 1, link)
                scale_layer1(b, 1, link)
                add_down(b, 6)
                hidden(b, 8)
                scale_weigh2(b, 0)
                scale_weigh2(b, 1)
                sum_layer2(b, 0)
                add_down(b, 7)
                need(dve, b, "xt_copied", 1)
                turned_by_dve(bank("x_turn", 0)).then_inc(sem["xt_split"], 1)
                add_down(b, 8)
                scale_weigh2(b, 2)
                scale_weigh2(b, 3)
                sum_layer2(b, 1)
                split_stack(b, 0)
                split_qm(b, PAIRS)
                split_stack(b, 1)
                split_qm(b, PAIRS + 1)
                for p in range(2, 8):
                    split_stack(b, p)
                assert count[0] == VECTOR_LINKS, count[0]
                count[0] = 0
            finish_stats(B, linker(B))
            finish_norm(B)

        @block.tensor
        def _(pe):
            def setup_bank(n):
                if n >= BANKS:
                    emptied(pe, n - BANKS)
                return setup_psum(n)

            pe.wait_ge(once["pool_setup"], 4)
            for n, kind in enumerate(SETUP):
                k = n - first[kind]
                dst = setup_bank(n)
                if kind == "x_turn":
                    pe.wait_ge(once["first_xa"], 1)
                    for j, src in enumerate((xa, xn)):
                        for t in range(T):
                            ins = pe.transpose(dst[:, (2 * j + t) * P:(2 * j + t + 1) * P], src[:, t, :], ident[:])
                elif kind == "w_turn":
                    if k == 0:
                        loaded(pe, "ld_q")
                    if k == 2:
                        loaded(pe, "ld_k")
                    if k == 4:
                        loaded(pe, "ld_v")
                    w = (wq, wk, wv)[k // 2]
                    for j in range(4):
                        p = 4 * (k % 2) + j
                        ins = pe.transpose(dst[:, j * P:(j + 1) * P], w[:, p * P:(p + 1) * P], ident[:])
                elif kind == "m":
                    if k == 0:
                        emptied(pe, first["w_turn"] + 3)
                    for j in range(4):
                        h = 8 * (k // 2) + 2 * j + k % 2
                        rows = slice(DH * (h % 2), DH * (h % 2) + DH)
                        ins = pe.matmul(dst[:, j * P:(j + 1) * P], wt[rows, 0, h // 2, :], wt[rows, 1, h // 2, :],
                                        start=True, stop=True)
                elif kind == "vw1":
                    if k == 0:
                        emptied(pe, first["w_turn"] + 5)
                    for j in range(4):
                        ins = pe.matmul(dst[:, j * P:(j + 1) * P], wt[:, 2, 4 * k + j, :], w1_2,
                                        start=True, stop=True)
                elif kind == "lin_turn":
                    loaded(pe, "ld_o")
                    ins = pe.transpose(dst[0:DH, 0:DH], lin_sb, ident[0:DH, 0:DH])
                elif kind == "lin_wo":
                    if k == 0:
                        emptied(pe, first["lin_turn"])
                    ins = pe.matmul(dst[DH:P, :], lin_t,
                                    wo_raw[:, 4 * k:4 * k + 4, :].rearrange("p h n -> p (h n)"),
                                    start=True, stop=True)
                else:
                    pe.wait_ge(once["wo_summed"], 4)
                    ins = pe.matmul(dst[:, 0:1], wo_part[:, 0, :], lin_b_col[:], start=True, stop=True)
                ins.then_inc(once["setup_product"], 1)
            pe.wait_ge(once["wg_split"], 1)

            def split_product(out, a, b, a_at, b_at, start=True, stop=True):
                pe.matmul(out, a_at(a[1]), b_at(b[0]), start=start, stop=False)
                pe.matmul(out, a_at(a[0]), b_at(b[1]), start=False, stop=False)
                return pe.matmul(out, a_at(a[0]), b_at(b[0]), start=False, stop=stop)

            whole = lambda w: w[:]

            def free_bank(b, n):
                m = n - BANKS
                while m < 0 and m + SLOTS >= len(JOBS):
                    m -= BANKS
                kind, i = JOBS[m if m >= 0 else m + SLOTS]
                if m >= 0:
                    need(pe, b, READ_BY[kind], i + 1)
                else:
                    need(pe, b, READ_BY[kind], max(i + 1 - PER_SEQ[READ_BY[kind]], 0))

            def product(b, kind, i):
                dst = bank(kind, 0 if kind == "out" else i)
                if kind == "gates":
                    if b is not None:
                        need(pe, b, "xt_split", 1)
                    for t in range(T):
                        ins = split_product(dst[:, t * 8:t * 8 + 8], xn_t, wg, lambda x: x[:, t * P:(t + 1) * P], whole)
                elif kind == "qm":
                    for j in range(2):
                        ins = split_product(dst[:, j * T * P:(j + 1) * T * P], m_w, xa_t,
                                            lambda w: w[:, 2 * (i % PAIRS) + j, :], whole)
                elif kind == "scores":
                    need(pe, b, "qm_split", i // 2 + 1)
                    at = lambda q: q[:, (i // 2) % 2, i % 2, :]
                    pe.matmul(dst[:, 0:P], at(qm0), xa_t0[:], start=True, stop=True)
                    ins = split_product(dst[:, P:3 * P], qm1, xa_t, at, whole)
                elif kind == "vh":
                    q, t = i // 2, i % 2
                    if i == 0:
                        pe.wait_ge(once["vh_w_split"], 1)
                    ins = split_product(dst, xa_t, vh_w, lambda x: x[:, t * P:(t + 1) * P],
                                        lambda w: w[:, 4 * q:4 * q + 4, :].rearrange("p h d -> p (h d)"))
                elif kind == "turn":
                    need(pe, b, "diag_set", i // 2 + 1)
                    for k in range(3):
                        ins = pe.transpose(dst[:, k * P:(k + 1) * P], ex[:, i % 4, k, :], ident[:])
                elif kind == "layer1":
                    need(pe, b, "et_copied", i + 1)
                    need(pe, b, "vh_copied", 2 * (i // 4) + 2)
                    pe.matmul(dst[:, 0:VHW], et[:, i, 0:P], vh[:, 0, i, :], start=True, stop=True)
                    pe.matmul(dst[:, VHW:2 * VHW], et[:, i, P:2 * P], vh[:, 0, i, :], start=True, stop=False)
                    ins = pe.matmul(dst[:, VHW:2 * VHW], et[:, i, 2 * P:3 * P], vh[:, 1, i, :],
                                    start=False, stop=True)
                elif kind in ("gate_up", "up"):
                    w = w_gate if kind == "gate_up" else w_up
                    if i == 0:
                        pe.wait_ge(once["shared_split"], 1)
                    if i == 1:
                        pe.wait_ge(once["ffn_w_split"], 2)
                    for c in range(C):
                        ins = split_product(dst[:, c * T * P:(c + 1) * T * P], w, xn_t,
                                            lambda w: w[:, i, c * P:(c + 1) * P], whole)
                elif kind == "down":
                    if i == 0:
                        loaded(pe, "ld_e")
                    need(pe, b, "hidden_made", i + 1)
                    for t in range(T):
                        for c in range(C):
                            ins = pe.matmul(dst[:, t * P:(t + 1) * P], hid[:, i % 2, (c * T + t) * P:(c * T + t + 1) * P],
                                            w_down[:, i, c, :], start=c == 0, stop=c == C - 1)
                elif kind == "layer2":
                    need(pe, b, "gelu1_done", i // 2 + 1)
                    for j in range(2):
                        for r in range(2):
                            h = 4 * i + 2 * j + r
                            rows = slice(DH * r, DH * r + DH)
                            at = j * T * P
                            pe.matmul(dst[rows, at:at + T * P], f1[:, 0, h, :], et[:, h, 0:2 * P],
                                      start=True, stop=False)
                            ins = pe.matmul(dst[rows, at + P:at + 2 * P], f1[:, 1, h, :], et[:, h, 2 * P:3 * P],
                                            start=False, stop=True)
                elif kind == "weigh2":
                    q, t = i // 2, i % 2
                    need(pe, b, "z_copied", 2 * q + 2)
                    for j in range(4):
                        ins = pe.matmul(dst[:, j * P:(j + 1) * P], zt[:, 4 * q + j, t * P:(t + 1) * P], w2_2[:],
                                        start=True, stop=True)
                elif kind == "stack":
                    need(pe, b, "gelu2_done", i // 4 + 1)
                    need(pe, b, "values_out", i // 4 + 1)
                    for j in range(2):
                        for t in range(T):
                            ins = pe.transpose(dst[:, (2 * j + t) * P:(2 * j + t + 1) * P],
                                               of[:, 2 * i + j, t, 0:2 * DH], ident[:])
                elif kind == "x_turn":
                    need(pe, b, "xa_done", 1)
                    for j, src in enumerate((xa, xn)):
                        for t in range(T):
                            ins = pe.transpose(dst[:, (2 * j + t) * P:(2 * j + t + 1) * P], src[:, t, :], ident[:])
                elif kind == "out":
                    if i == 0:
                        pe.wait_ge(once["o_w_split"], 1)
                    need(pe, b, "stack_split", i + 1)
                    for j in range(2):
                        ins = split_product(dst[:, 0:T * P], o_w, of_t, lambda w: w[:, 2 * i + j, :],
                                            lambda x: x[:, i % STACKS, j * T * P:(j + 1) * T * P],
                                            start=(i, j) == (0, 0), stop=(i, j) == (PAIRS - 1, 1))
                elif kind == "out_turn":
                    need(pe, b, "y_copied", 0)
                    for t in range(T):
                        ins = pe.transpose(dst[:, t * P:(t + 1) * P], y_t[:, t * P:(t + 1) * P], ident[:])
                return ins

            pe.wait_ge(once["counters_set"], 1)
            ahead = [("gates", 1), ("qm", PAIRS), ("qm", PAIRS + 1), ("scores", H), ("scores", H + 1)]
            for n, (kind, i) in enumerate(ahead):
                for other, j in ahead[:n]:
                    if (slot[kind, i] - slot[other, j]) % BANKS == 0:
                        need(pe, None, READ_BY[other], j + 1)
                emptied(pe, max(m for m in range(len(SETUP)) if (slot[kind, i] - m - SHIFT) % BANKS == 0))
                product(None, kind, i).then_inc(sem[kind], 1)
            emptied(pe, len(SETUP) - 1)
            with pe.Fori(0, B) as b:
                for kind, i in ORDER:
                    if (kind, i) in slot:
                        free_bank(b, slot[kind, i])
                    product(b, kind, i).then_inc(sem[kind], 1)
            product(B, "out_turn", 0).then_inc(sem["out_turn"], 1)


_INS = ["x", "gamma_in", "Wq", "Wk", "Wv", "gnn_w", "gnn_b", "lin_w", "lin_b", "Wo", "gamma_out"]
_FFN = ["Wg", "Ws1", "Ws3", "Ws2", "We1", "We3", "We2"]


def kernel(**inputs):
    import numpy as np
    import concourse.bacc as bacc
    from concourse.bass_utils import run_bass_kernel_spmd

    nc = bacc.Bacc("TRN2", target_bir_lowering=False, num_devices=1)
    arrays, args = {}, []
    for name in ["L0_attn_" + n for n in _INS] + ["L0_ffn_" + n for n in _FFN]:
        a = np.ascontiguousarray(inputs[name])
        arrays[f"in_{name}"] = a
        args.append(nc.dram_tensor(f"in_{name}", a.shape, mybir.dt.from_np(a.dtype), kind="ExternalInput").ap())
    out = nc.dram_tensor("out", inputs["L0_attn_x"].shape, F32, kind="ExternalOutput").ap()
    build(nc, *args, out)
    r = run_bass_kernel_spmd(nc, [arrays], core_ids=[0])
    return r.results[0]["out"]
```
